# Optimizing a Trainium2 kernel written in Bass

```python
import numpy as np
import jax
import jax.numpy as jnp

def _softmax(x, axis=-1):
    return jax.nn.softmax(x, axis=axis)

def _gelu(x):
    return jax.nn.gelu(x, approximate=True)

def _silu(x):
    return jax.nn.silu(x)

def _sigmoid(x):
    return jax.nn.sigmoid(x)

def _layernorm(x, axis=-1, eps=1e-05):
    m = jnp.mean(x, axis=axis, keepdims=True)
    v = jnp.var(x, axis=axis, keepdims=True)
    return (x - m) / jnp.sqrt(v + eps)

def _scatter_add(tgt, idx, src, axis=0):
    return tgt.at[idx].add(src)

def _segment_sum(src, seg, n):
    return jax.ops.segment_sum(src, seg, n)
kernel_name = 'mk_gnn_resnorm_d4_gnn_r64_6fbe6c'

def setup_inputs(seed: int=0):
    np.random.seed(seed)
    _w = jnp.asarray

    def _rec_inputs():
        import jax
        import jax.numpy as jnp
        _gk = jax.random.key(seed)
        x = -0.0005121 + 1.001 * jax.random.normal(jax.random.fold_in(_gk, 1), (100000, 32), jnp.float32)
        src = jax.random.randint(jax.random.fold_in(_gk, 2), (50000,), 0, 100000, jnp.int32)
        dst = jax.random.randint(jax.random.fold_in(_gk, 3), (50000,), 0, 100000, jnp.int32)
        _o = jnp.argsort(dst, stable=True)
        src = src[_o]
        dst = dst[_o]
        edge_attr_10 = jax.random.uniform(jax.random.fold_in(_gk, 12), (50000, 10), jnp.float32, 0.0, 0.999998)
        edge_attr_3 = 0.00158508 + 0.999651 * jax.random.normal(jax.random.fold_in(_gk, 13), (50000, 3), jnp.float32)
        edge_weight = jax.random.uniform(jax.random.fold_in(_gk, 15), (50000,), jnp.float32, 0.0, 0.999997)
        return (x, src, dst, edge_attr_10, edge_attr_3, edge_weight)
    x, src, dst, edge_attr_10, edge_attr_3, edge_weight = _rec_inputs()

    def _L0_gnn_setup():
        import jax, jax.numpy as jnp
        import numpy as np
        N_NODES = 100000
        N_EDGES = 25000
        D_FEAT = 32
        EPS = 1e-12
        key = jax.random.key(seed)
        k1, k2, k3 = jax.random.split(key, 3)
        feat = jax.random.normal(k1, (N_NODES, D_FEAT), dtype=jnp.float32)
        beta = jnp.ones((1,), dtype=jnp.float32)
        src = jax.random.randint(k2, (N_EDGES,), 0, N_NODES, dtype=jnp.int32)
        dst = jax.random.randint(k3, (N_EDGES,), 0, N_NODES, dtype=jnp.int32)
        return {'feat': feat, 'beta': beta, 'src': src, 'dst': dst}
    _L0_gnn_all = _L0_gnn_setup()
    _L0_gnn_in = {k: v for k, v in _L0_gnn_all.items() if k in ('beta',)}
    del _L0_gnn_all

    def _L1_gnn_setup():
        import jax, jax.numpy as jnp
        import numpy as np
        N_NODES = 50000
        N_EDGES = 12500
        C_IN = 32
        C_OUT = 32
        BN_EPS = 1e-05

        def batch_norm(h, gamma, beta):
            mean = jnp.mean(h, axis=0)
            var = jnp.mean((h - mean) ** 2, axis=0)
            return (h - mean) * jax.lax.rsqrt(var + BN_EPS) * gamma + beta
        key = jax.random.key(seed)
        ks = jax.random.split(key, 8)
        x = jax.random.normal(ks[0], (N_NODES, C_IN), dtype=jnp.float32)
        edge_index = jax.random.randint(ks[1], (2, N_EDGES), 0, N_NODES, dtype=jnp.int64)
        s1 = 1.0 / np.sqrt(2 * C_IN)
        s2 = 1.0 / np.sqrt(C_OUT)
        W1 = jax.random.uniform(ks[2], (2 * C_IN, C_OUT), jnp.float32, -s1, s1)
        b1 = jax.random.uniform(ks[3], (C_OUT,), jnp.float32, -s1, s1)
        W2 = jax.random.uniform(ks[4], (C_OUT, C_OUT), jnp.float32, -s2, s2)
        b2 = jax.random.uniform(ks[5], (C_OUT,), jnp.float32, -s2, s2)
        gamma1 = jnp.ones((C_OUT,), jnp.float32)
        beta1 = jnp.zeros((C_OUT,), jnp.float32)
        gamma2 = jnp.ones((C_OUT,), jnp.float32)
        beta2 = jnp.zeros((C_OUT,), jnp.float32)
        return {'x': x, 'W1': W1, 'b1': b1, 'gamma1': gamma1, 'beta1': beta1, 'W2': W2, 'b2': b2, 'gamma2': gamma2, 'beta2': beta2, 'edge_index': edge_index}
    _L1_gnn_all = _L1_gnn_setup()
    _L1_gnn_in = {k: v for k, v in _L1_gnn_all.items() if k in ('W1', 'b1', 'gamma1', 'beta1', 'W2', 'b2', 'gamma2', 'beta2')}
    del _L1_gnn_all

    def _L2_gnn_setup():
        import jax, jax.numpy as jnp
        import numpy as np
        K = 10
        ALPHA = 0.1
        BETA = 0.9
        N_NODES = 100000
        N_EDGES = 25000
        D_FEAT = 32
        key = jax.random.key(seed)
        k1, k2 = jax.random.split(key)
        x = jax.random.normal(k1, (N_NODES, D_FEAT), dtype=jnp.float32)
        edge_index = jax.random.randint(k2, (2, N_EDGES), 0, N_NODES, dtype=jnp.int64)
        return {'x': x, 'edge_index': edge_index}
    _L2_gnn_all = _L2_gnn_setup()
    _L2_gnn_in = {k: v for k, v in _L2_gnn_all.items() if k in ()}
    del _L2_gnn_all

    def _L3_gnn_setup():
        import jax, jax.numpy as jnp
        import numpy as np
        SQRT3 = 3.0 ** 0.5

        def _mlp(emb, w1, w2):
            h = jax.nn.relu(emb @ w1 / jnp.sqrt(jnp.float32(w1.shape[0])))
            return h @ w2 / jnp.sqrt(jnp.float32(w2.shape[0]))
        key = jax.random.key(seed)
        ks = jax.random.split(key, 10)
        N, E = (10000, 2500)
        x = jax.random.normal(ks[0], (N, 32), jnp.float32)
        edge_src = jax.random.randint(ks[1], (E,), 0, N)
        edge_dst = jax.random.randint(ks[2], (E,), 0, N)
        edge_vec = jax.random.normal(ks[3], (E, 3), jnp.float32)
        emb = jax.random.uniform(ks[4], (E, 10), jnp.float32)
        norm = jax.random.uniform(ks[5], (E,), jnp.float32)
        fc1_w1 = jax.random.normal(ks[6], (10, 16), jnp.float32)
        fc1_w2 = jax.random.normal(ks[7], (16, 512), jnp.float32)
        fc2_w1 = jax.random.normal(ks[8], (10, 16), jnp.float32)
        fc2_w2 = jax.random.normal(ks[9], (16, 384), jnp.float32)
        return dict(x=x, edge_src=edge_src, edge_dst=edge_dst, edge_vec=edge_vec, emb=emb, norm=norm, num_nodes=N, fc1_w1=fc1_w1, fc1_w2=fc1_w2, fc2_w1=fc2_w1, fc2_w2=fc2_w2)
    _L3_gnn_all = _L3_gnn_setup()
    _L3_gnn_in = {k: v for k, v in _L3_gnn_all.items() if k in ('fc1_w1', 'fc1_w2', 'fc2_w1', 'fc2_w2')}
    del _L3_gnn_all
    return {'x': x, 'src': src, 'dst': dst, 'edge_attr_10': edge_attr_10, 'edge_attr_3': edge_attr_3, 'edge_weight': edge_weight, 'L0_gnn_beta': _L0_gnn_in['beta'], 'L1_gnn_W1': _L1_gnn_in['W1'], 'L1_gnn_b1': _L1_gnn_in['b1'], 'L1_gnn_gamma1': _L1_gnn_in['gamma1'], 'L1_gnn_beta1': _L1_gnn_in['beta1'], 'L1_gnn_W2': _L1_gnn_in['W2'], 'L1_gnn_b2': _L1_gnn_in['b2'], 'L1_gnn_gamma2': _L1_gnn_in['gamma2'], 'L1_gnn_beta2': _L1_gnn_in['beta2'], 'L3_gnn_fc1_w1': _L3_gnn_in['fc1_w1'], 'L3_gnn_fc1_w2': _L3_gnn_in['fc1_w2'], 'L3_gnn_fc2_w1': _L3_gnn_in['fc2_w1'], 'L3_gnn_fc2_w2': _L3_gnn_in['fc2_w2']}

def reference(x, src, dst, edge_attr_10, edge_attr_3, edge_weight, L0_gnn_beta, L1_gnn_W1, L1_gnn_b1, L1_gnn_gamma1, L1_gnn_beta1, L1_gnn_W2, L1_gnn_b2, L1_gnn_gamma2, L1_gnn_beta2, L3_gnn_fc1_w1, L3_gnn_fc1_w2, L3_gnn_fc2_w1, L3_gnn_fc2_w2):
    import jax
    import jax.numpy as jnp

    def _L0_gnn_ref(feat, beta, src, dst):
        import jax, jax.numpy as jnp
        import numpy as np
        N_NODES = 100000
        N_EDGES = 25000
        D_FEAT = 32
        EPS = 1e-12
        N = feat.shape[0]
        norm = jnp.maximum(jnp.linalg.norm(feat, axis=-1, keepdims=True), EPS)
        norm_h = feat / norm
        cos = jnp.sum(norm_h[src] * norm_h[dst], axis=-1)
        e = beta[0] * cos
        m = jax.lax.stop_gradient(jax.ops.segment_max(e, dst, num_segments=N))
        m = jnp.where(jnp.isfinite(m), m, 0.0)
        p = jnp.exp(e - m[dst])
        s = jax.ops.segment_sum(p, dst, num_segments=N)
        p = p / s[dst]
        out = jax.ops.segment_sum(feat[src] * p[:, None], dst, num_segments=N)
        return out

    def _L1_gnn_ref(x, W1, b1, gamma1, beta1, W2, b2, gamma2, beta2, edge_index):
        import jax, jax.numpy as jnp
        import numpy as np
        N_NODES = 50000
        N_EDGES = 12500
        C_IN = 32
        C_OUT = 32
        BN_EPS = 1e-05

        def batch_norm(h, gamma, beta):
            mean = jnp.mean(h, axis=0)
            var = jnp.mean((h - mean) ** 2, axis=0)
            return (h - mean) * jax.lax.rsqrt(var + BN_EPS) * gamma + beta
        row, col = (edge_index[0], edge_index[1])
        ef = jnp.concatenate([x[row], x[col]], axis=-1)
        h = jax.nn.relu(batch_norm(ef @ W1 + b1, gamma1, beta1))
        h = jax.nn.relu(batch_norm(h @ W2 + b2, gamma2, beta2))
        out = jax.ops.segment_sum(h, row, num_segments=x.shape[0])
        return out

    def _L2_gnn_ref(x, edge_index):
        import jax, jax.numpy as jnp
        import numpy as np
        K = 10
        ALPHA = 0.1
        BETA = 0.9
        N_NODES = 100000
        N_EDGES = 25000
        D_FEAT = 32
        n = x.shape[0]
        row, col = (edge_index[0], edge_index[1])
        ones = jnp.ones(row.shape[0], dtype=x.dtype)
        deg = jax.ops.segment_sum(ones, row, num_segments=n)
        deg = jnp.maximum(deg, jnp.asarray(1.0, x.dtype))
        w = jax.lax.rsqrt(deg[row] * deg[col])
        h = x
        out = h
        for _ in range(K):
            msg = w[:, None] * out[col]
            out = jax.ops.segment_sum(msg, row, num_segments=n)
            out = out * BETA + h * ALPHA
        gamma = BETA ** K + ALPHA * sum((BETA ** i for i in range(K)))
        return out / jnp.asarray(gamma, x.dtype)

    def _L3_gnn_ref(x, edge_src, edge_dst, edge_vec, emb, norm, num_nodes, fc1_w1, fc1_w2, fc2_w1, fc2_w2):
        import jax, jax.numpy as jnp
        import numpy as np
        SQRT3 = 3.0 ** 0.5

        def _mlp(emb, w1, w2):
            h = jax.nn.relu(emb @ w1 / jnp.sqrt(jnp.float32(w1.shape[0])))
            return h @ w2 / jnp.sqrt(jnp.float32(w2.shape[0]))
        E = edge_vec.shape[0]
        r = edge_vec / jnp.linalg.norm(edge_vec, axis=1, keepdims=True)
        sh1 = SQRT3 * r
        xs, xd = (x[edge_src], x[edge_dst])
        s1 = jnp.concatenate([xs[:, :8], xd[:, :8]], axis=1)
        v1 = jnp.concatenate([xs[:, 8:].reshape(E, 8, 3), xd[:, 8:].reshape(E, 8, 3)], axis=1)
        w = _mlp(emb, fc1_w1, fc1_w2)
        Wss = w[:, 0:128].reshape(E, 16, 8)
        Wvv = w[:, 128:256].reshape(E, 16, 8)
        Wsv = w[:, 256:384].reshape(E, 16, 8)
        Wvs = w[:, 384:512].reshape(E, 16, 8)
        a1 = 1.0 / jnp.sqrt(32.0)
        vdot1 = jnp.einsum('euk,ek->eu', v1, sh1) / SQRT3
        s_t = a1 * (jnp.einsum('eu,euw->ew', s1, Wss) + jnp.einsum('eu,euw->ew', vdot1, Wvv))
        v_t = a1 * (jnp.einsum('eu,euw->ew', s1, Wsv)[:, :, None] * sh1[:, None, :] + jnp.einsum('euk,euw->ewk', v1, Wvs))
        w2 = _mlp(emb, fc2_w1, fc2_w2)
        Ass = w2[:, 0:64].reshape(E, 8, 8)
        Avv = w2[:, 64:128].reshape(E, 8, 8)
        Bss = w2[:, 128:192].reshape(E, 8, 8)
        Bvv = w2[:, 192:256].reshape(E, 8, 8)
        Csv = w2[:, 256:320].reshape(E, 8, 8)
        Cvs = w2[:, 320:384].reshape(E, 8, 8)
        a2 = 1.0 / jnp.sqrt(16.0)
        vdot2 = jnp.einsum('euk,ek->eu', v_t, sh1) / SQRT3
        scal = a2 * (jnp.einsum('eu,euw->ew', s_t, Ass) + jnp.einsum('eu,euw->ew', vdot2, Avv))
        gates = a2 * (jnp.einsum('eu,euw->ew', s_t, Bss) + jnp.einsum('eu,euw->ew', vdot2, Bvv))
        vecs = a2 * (jnp.einsum('eu,euw->ew', s_t, Csv)[:, :, None] * sh1[:, None, :] + jnp.einsum('euk,euw->ewk', v_t, Cvs))
        edge_out = jnp.concatenate([jnp.tanh(scal), (vecs * jnp.tanh(gates)[:, :, None]).reshape(E, 24)], axis=1)
        edge_out = edge_out * norm[:, None]
        return jax.ops.segment_sum(edge_out, edge_dst, num_segments=num_nodes)
    edge_index = jnp.stack([src, dst])
    x = _layernorm(x + _L0_gnn_ref(x, L0_gnn_beta, src, dst), axis=-1)
    x = _layernorm(x + _L1_gnn_ref(x, L1_gnn_W1, L1_gnn_b1, L1_gnn_gamma1, L1_gnn_beta1, L1_gnn_W2, L1_gnn_b2, L1_gnn_gamma2, L1_gnn_beta2, edge_index), axis=-1)
    x = _layernorm(x + _L2_gnn_ref(x, edge_index), axis=-1)
    x = _layernorm(x + _L3_gnn_ref(x, src, dst, edge_attr_3, edge_attr_10, edge_weight, 100000, L3_gnn_fc1_w1, L3_gnn_fc1_w2, L3_gnn_fc2_w1, L3_gnn_fc2_w2), axis=-1)
    return x

_drawn_inputs = setup_inputs


def setup_inputs(seed=0):
    import zlib

    import numpy as np

    out = dict(_drawn_inputs(seed))
    spreads = {'L1_gnn_gamma1': (1.0, 0.2),
     'L1_gnn_beta1': (0.0, 0.1),
     'L1_gnn_gamma2': (1.0, 0.2),
     'L1_gnn_beta2': (0.0, 0.1)}
    factors = {'edge_weight': 2.797, 'L1_gnn_b1': 8.0, 'L1_gnn_b2': 8.0}
    for name, (base, spread) in spreads.items():
        noise = np.random.default_rng([zlib.crc32(name.encode()), seed]).standard_normal(out[name].shape)
        drawn = base * np.exp(spread * noise) if base else spread * noise
        out[name] = jnp.asarray(drawn.astype(out[name].dtype))
    for name, factor in factors.items():
        out[name] = (out[name] * factor).astype(out[name].dtype)
    return out
```

```python
import numpy as np
import concourse.bass as bass
from concourse import mybir
from concourse.alu_op_type import AluOpType as ALU
from contextlib import ExitStack, contextmanager

F32 = mybir.dt.float32
I32 = mybir.dt.int32
ACT = mybir.ActivationFunctionType
AX = mybir.AxisListType.X

P = 128
N = 100000
E = 50000
D = 32
J = 392
EP = P * J
C = 28
NCH = J // C
HALF = NCH // 2
CD = C * D
SORTW = 512
SORTP = EP // SORTW
LOG = 16
R = 32
NODES_CH = P * R
DENSE = N // NODES_CH
TAILP = (N - DENSE * NODES_CH) // R
LNEPS = 1e-5
BNEPS = 1e-5
BIG = 3.0e38
KSTEPS = 10
ALPHA, BETA = 0.1, 0.9
GAMMA = BETA ** KSTEPS + ALPHA * sum(BETA ** i for i in range(KSTEPS))
MAXROW = N - 1


class Chain:

    def __init__(self, engine, sem):
        self.engine, self.sem, self.k, self.terms = engine, sem, 0, []

    def value(self):
        v = self.k
        for i, start, per in self.terms:
            v = i * per + v - start * per
        return v

    def tick(self, ins):
        ins.then_inc(self.sem, 1)
        self.k += 1

    def link(self, ins):
        self.tick(ins)
        self.engine.wait_ge(self.sem, self.value())

    @contextmanager
    def loop(self, start, end, per):
        k0 = self.k
        with self.engine.Fori(start, end) as i:
            self.terms.append((i, start, per))
            yield i
            assert self.k - k0 == per, (self.k - k0, per)
            self.terms.pop()
        self.k = k0 + (end - start) * per


def cols(t, c, width=1):
    return t[:, bass.ds(c * (C * width), C * width)]


def copy(nc, out, in_):
    return nc.vector.tensor_scalar(out, in_, 1.0, None, ALU.mult)


def rows3(ap, d=D):
    return ap.rearrange("p (j f) -> p j f", f=d)


def spread(ap, d=D):
    n = ap.shape[1]
    return ap.rearrange("p (n a) -> p n a", a=1).broadcast_to([ap.shape[0], n, d])


def repeat(ap, n):
    return ap.rearrange("p (a d) -> p a d", a=1).broadcast_to([ap.shape[0], n, ap.shape[1]])


def build(nc, x, src_pe, dst_pe, dst_prev, dst_next, attr3, attr10t, weight, beta, W1, W2, vecs,
          fc1_w1, fc1_w2, fc2_w1, fc2_w2, out):
    T1 = nc.dram_tensor("T1", (N, D), F32, kind="Internal").ap()
    T2 = nc.dram_tensor("T2", (N, D), F32, kind="Internal").ap()
    T3 = nc.dram_tensor("T3", (N, D), F32, kind="Internal").ap()
    NT = nc.dram_tensor("NT", (P * 784, 2), F32, kind="Internal").ap()
    U = nc.dram_tensor("U", (EP + 1, D), F32, kind="Internal").ap()
    sorted_src = nc.dram_tensor("sorted_src", (EP + 2,), F32, kind="Internal").ap()
    sorted_dst = nc.dram_tensor("sorted_dst", (EP,), F32, kind="Internal").ap()
    top = ExitStack()

    def sb(ctx, name, shape, dt=F32):
        return ctx.enter_context(nc.sbuf_tensor(name, shape, dt))

    def ps(ctx, name, shape, dt=F32):
        return ctx.enter_context(nc.psum_tensor(name, shape, dt))

    live = []
    begun = nc.alloc_semaphore(name="begun")

    def sem(ctx, name):
        live.append(nc.alloc_semaphore(name=name))
        return live[-1]

    def recycle():
        nc.clear_and_free_semaphores(live)
        live.clear()
        nc.all_engine_barrier()

    with top:
        R1 = sb(top, "R1", [P, J * D])
        R2 = sb(top, "R2", [P, J * D])
        lay = ExitStack()
        slots = [sb(top, f"slot{s}", [P, C * 2 * D]) for s in range(2)]
        islots = [sb(top, f"islot{s}", [P, 2 * C], I32) for s in range(2)]
        ident = sb(top, "ident", [P, P])
        ones = sb(top, "ones", [P, P])
        pos = sb(top, "pos", [P, J])
        contD, nendD, FD = (sb(top, n, [P, J]) for n in ("contD", "nendD", "FD"))
        sidxD, srcD, dstD = (sb(top, n, [P, J], I32) for n in ("sidxD", "srcD", "dstD"))
        ATD = sb(top, "ATD", [D, P])
        carry = sb(top, "carry", [P, D])
        crow = sb(top, "crow", [D, P + 1])
        vec = sb(top, "vec", [P, 7 * D])
        b1v, g1v, be1v, b2v, g2v, be2v = (vec[:, i * D:(i + 1) * D] for i in range(6))
        betav = vec[:, 6 * D:6 * D + 1]
        R3 = sb(lay, "R3", [P, (J + 1) * D])
        SCRATCH = 5120


        def dense_act(act, eps, src_t, dst_t, s, din, dout, tmp):
            dst_v = dst_t[0:DENSE * NODES_CH, :].rearrange("(k p r) f -> k p (r f)", p=P, r=R)
            src_v = src_t[0:DENSE * NODES_CH, :].rearrange("(k p r) f -> k p (r f)", p=P, r=R)
            dst_l = dst_t[DENSE * NODES_CH:N, :].rearrange("(p r) f -> p (r f)", r=R)
            src_l = src_t[DENSE * NODES_CH:N, :].rearrange("(p r) f -> p (r f)", r=R)
            ld, var_ready, std_ready, y_ready, st = s
            var, std = tmp

            def root(k, q, np_=P):
                act.wait_ge(var_ready, k + 1)
                nc.scalar.activation(std[0:np_, :], var[0:np_, :], ACT.Sqrt, bias=eps[0:np_, :],
                                     scale=1.0 / D).then_inc(std_ready, 1)
                act.wait_ge(y_ready, k + 1)

            act.dma_start(din[0][:, :], src_v[0]).then_inc(ld[0], 16)
            act.dma_start(din[1][:, :], src_v[1]).then_inc(ld[1], 16)
            with act.Fori(0, DENSE // 2 - 1) as i:
                for q in range(2):
                    k = i * 2 + q
                    root(k, q)
                    act.dma_start(dst_v[bass.ds(k, 1)].rearrange("a p n -> (a p) n"), dout[q][:, :]).then_inc(st[q], 16)
                    act.dma_start(din[q][:, :], src_v[bass.ds(k + 2, 1)].rearrange("a p n -> (a p) n")).then_inc(ld[q], 16)
            root(DENSE - 2, 0)
            act.dma_start(dst_v[DENSE - 2], dout[0][:, :]).then_inc(st[0], 16)
            act.dma_start(din[0][0:TAILP, :], src_l).then_inc(ld[0], 16)
            root(DENSE - 1, 1)
            act.dma_start(dst_v[DENSE - 1], dout[1][:, :]).then_inc(st[1], 16)
            root(DENSE, 0, TAILP)
            act.dma_start(dst_l, dout[0][0:TAILP, :]).then_inc(st[0], 16)
            act.wait_ge(st[0], 16 * (DENSE // 2 + 1))
            act.wait_ge(st[1], 16 * (DENSE // 2))

        def dense_dve(dve, ch, s, din, dout, tmp, small):
            ld, var_ready, std_ready, y_ready, st = s
            var, std = tmp
            total, rstd, centred, sq = small

            def chunk(i, q, first=False, np_=P):
                dve.wait_ge(ld[q], i * 16 + 16)
                xin = rows3(din[q][0:np_, :])
                ch.link(nc.vector.tensor_reduce(total[0:np_, :], xin, AX, ALU.add))
                ch.link(nc.vector.scalar_tensor_tensor(rows3(centred[0:np_, :]), spread(total[0:np_, :]),
                                                       -1.0 / D, xin, ALU.mult, ALU.add))
                ch.link(nc.vector.tensor_tensor(sq[0:np_, :], centred[0:np_, :], centred[0:np_, :], ALU.mult))
                nc.vector.tensor_reduce(var[0:np_, :], rows3(sq[0:np_, :]), AX, ALU.add).then_inc(var_ready, 1)
                dve.wait_ge(std_ready, i * 2 + q + 1)
                ch.link(nc.vector.reciprocal(rstd[0:np_, :], std[0:np_, :]))
                if not first:
                    dve.wait_ge(st[q], i * 16)
                nc.vector.tensor_tensor(rows3(dout[q][0:np_, :]), rows3(centred[0:np_, :]),
                                        spread(rstd[0:np_, :]), ALU.mult).then_inc(y_ready, 1)
                dve.wait_ge(y_ready, i * 2 + q + 1)

            chunk(0, 0, first=True)
            chunk(0, 1, first=True)
            with ch.loop(1, DENSE // 2, 8) as i:
                chunk(i, 0)
                chunk(i, 1)
            chunk(DENSE // 2, 0, np_=TAILP)

        @contextmanager
        def dense_buffers(ctx, tag):
            at = [SCRATCH]

            def part(n):
                at[0] += n
                return R3[:, at[0] - n:at[0]]

            din, dout = [part(R * D), part(R * D)], [part(R * D), part(R * D)]
            tmp = (part(R), part(R))
            small = (part(R), part(R), part(R * D), part(R * D))
            s = ([sem(ctx, f"dense_ld{q}_{tag}") for q in range(2)], sem(ctx, f"dense_var_{tag}"),
                 sem(ctx, f"dense_std_{tag}"), sem(ctx, f"dense_y_{tag}"),
                 [sem(ctx, f"dense_st{q}_{tag}") for q in range(2)])
            yield din, dout, tmp, small, s

        def stage_indices(sp, taken, staged, index_tiles):
            with sp.Fori(0, HALF) as i:
                for q in range(2):
                    sp.wait_ge(taken, i * 2 + q + 1)
                    for n, t in enumerate(index_tiles):
                        sp.dma_start(islots[q][:, n * C:(n + 1) * C], cols(t, i * 2 + q)).then_inc(staged[q], 16)

        def gather(pool, i, q, got, tables, width, per, stride=None):
            stride = stride or width * len(tables)
            for j in range(C):
                for n, t in enumerate(tables):
                    o = j * stride + n * width
                    pool.indirect_dma_start(slots[q][:, o:o + width], None, t,
                                            bass.IndirectOffsetOnAxis(ap=islots[q][:, n * C + j:n * C + j + 1], axis=0),
                                            bounds_check=per, oob_is_err=False).then_inc(got[q], 16)

        def gather_pass(pool, staged, got, tables, width, limit):
            limit = pool.to_reg(limit)
            with pool.Fori(0, HALF) as i:
                for q in range(2):
                    pool.wait_ge(staged[q], i * (16 * len(tables)) + 16 * len(tables))
                    pool.sem_inc(begun, 1)
                    gather(pool, i, q, got, tables, width, limit)

        def scatter_pass(pool, filled, sent, table, width):
            limit = pool.to_reg(MAXROW)
            with pool.Fori(0, HALF) as i:
                for q in range(2):
                    pool.wait_ge(filled, i * 2 + q + 1)
                    pool.sem_inc(begun, 1)
                    for j in range(C):
                        pool.indirect_dma_start(table, bass.IndirectOffsetOnAxis(ap=islots[q][:, j:j + 1], axis=0),
                                                slots[q][:, j * width:(j + 1) * width], None,
                                                bounds_check=limit, oob_is_err=False).then_inc(sent[q], 16)
            for q in range(2):
                pool.wait_ge(sent[q], 16 * C * HALF)

        def feature_scan(ch, cont, m, Rs):
            for f in range(D):
                ins = nc.vector.tensor_tensor_scan(Rs[:, D + f:D + f + (J - 1) * D + 1:D], cont[:, :],
                                                   m[:, f:f + (J - 1) * D + 1:D], 0.0, ALU.mult, ALU.add)
                ch.tick(ins)
            dve = ch.engine
            dve.wait_ge(ch.sem, ch.value())

        def chain_sems(ctx, tag):
            return [sem(ctx, f"{n}_{tag}") for n in ("last_ready", "row_ready", "chained", "back")]

        def carries_dve(ch, s, n, w, AT, pst, psb, dst, op0, op1, start, backward=False):
            dve = ch.engine
            _, row_ready, chained, back = s
            dve.wait_ge(row_ready, n + 1)
            if backward:
                ch.link(nc.vector.memset(crow[0:w, P:P + 1], start))
                nc.vector.tensor_tensor_scan(crow[0:w, P - 1::-1], AT[0:w, P - 1::-1], pst[0:w, P - 1::-1],
                                             start, op0, op1).then_inc(chained, 1)
            else:
                ch.link(nc.vector.memset(crow[0:w, 0:1], start))
                nc.vector.tensor_tensor_scan(crow[0:w, 1:P + 1], AT[0:w, :], pst[0:w, :],
                                             start, op0, op1).then_inc(chained, 1)
            dve.wait_ge(back, n + 1)
            ch.link(nc.vector.tensor_copy(dst, psb[:, 0:w]))

        def carries_pe(pe, s, n, w, last, pst, psb, backward=False):
            last_ready, row_ready, chained, back = s
            pe.wait_ge(last_ready, n + 1)
            nc.tensor.transpose(pst[0:w, :], last, ident[:, :]).then_inc(row_ready, 1)
            pe.wait_ge(chained, n + 1)
            o = 1 if backward else 0
            if isinstance(n, int):
                nc.tensor.transpose(psb[:, 0:w], crow[0:w, o:o + P], ident[0:w, 0:w]).then_inc(back, 1)
            else:
                nc.tensor.matmul(psb[:, 0:w], crow[0:w, o:o + P], ident[0:w, 0:w], start=True,
                                 stop=True).then_inc(back, 1)

        def flags_dve(ch, key, prev, nxt, cont, nend, F, sidx, tmp):
            ch.link(nc.vector.tensor_tensor(cont[:, :], key, prev, ALU.is_equal))
            ch.link(nc.vector.tensor_tensor(nend[:, :], key, nxt, ALU.is_equal))
            ch.link(nc.vector.tensor_tensor_scan(F[:, :], cont[:, :], cont[:, :], 1.0, ALU.mult, ALU.min))
            ch.link(nc.vector.tensor_scalar(tmp[:, :], key, -1.0, float(N), ALU.mult, ALU.add))
            ch.link(nc.vector.tensor_tensor(tmp[:, :], tmp[:, :], nend[:, :], ALU.mult))
            ch.link(nc.vector.tensor_tensor(tmp[:, :], tmp[:, :], key, ALU.add))
            ch.link(nc.vector.tensor_copy(sidx[:, :], tmp[:, :]))

        def finish(tag, own, Rs, F, sidx, table, own_scale=1.0, sum_scale=None, rowscale=None, keep=False,
                   extra=None):
            with ExitStack() as ctx:
                filled = sem(ctx, f"filled_{tag}")
                var_ready, std_ready = sem(ctx, f"var_{tag}"), sem(ctx, f"std_{tag}")
                sent = [sem(ctx, f"sent{q}_{tag}") for q in range(2)]
                step = sem(ctx, f"dve_{tag}")
                t = sb(ctx, f"t_{tag}", [P, CD])
                sq = sb(ctx, f"sq_{tag}", [P, CD])
                tot, var, std, rstd, eps = (sb(ctx, f"{n}_{tag}", [P, C]) for n in ("tot", "var", "std", "rstd", "eps"))
                block = ctx.enter_context(nc.Block())

                @block.gpsimd
                def _(pool):
                    scatter_pass(pool, filled, sent, table, D)

                @block.scalar
                def _(act):
                    act.wait_ge(step, 1)
                    with act.Fori(0, NCH) as c:
                        act.wait_ge(var_ready, c + 1)
                        nc.scalar.activation(std[:, :], var[:, :], ACT.Sqrt, bias=eps[:, 0:1],
                                             scale=1.0 / D).then_inc(std_ready, 1)

                @block.vector
                def _(dve):
                    ch = Chain(dve, step)
                    ch.link(nc.vector.memset(eps[:, :], LNEPS))

                    def chunk(i, q, first=False):
                        c = i * 2 + q
                        ch.link(nc.vector.tensor_tensor(rows3(t[:, :]), spread(cols(F, c)), repeat(carry[:, :], C), ALU.mult))
                        ch.link(nc.vector.tensor_tensor(t[:, :], t[:, :], Rs[:, bass.ds(c * CD + D, CD)], ALU.add))
                        if rowscale is not None:
                            ch.link(nc.vector.tensor_tensor(rows3(t[:, :]), rows3(t[:, :]), spread(cols(rowscale, c)), ALU.mult))
                        if sum_scale is not None:
                            ch.link(nc.vector.tensor_scalar(t[:, :], t[:, :], sum_scale, None, ALU.mult))
                        ch.link(nc.vector.scalar_tensor_tensor(t[:, :], cols(own, c, D), own_scale, t[:, :], ALU.mult, ALU.add))
                        ch.link(nc.vector.tensor_reduce(tot[:, :], rows3(t[:, :]), AX, ALU.add))
                        ch.link(nc.vector.scalar_tensor_tensor(rows3(t[:, :]), spread(tot[:, :]), -1.0 / D, rows3(t[:, :]), ALU.mult, ALU.add))
                        ch.link(nc.vector.tensor_tensor(sq[:, :], t[:, :], t[:, :], ALU.mult))
                        nc.vector.tensor_reduce(var[:, :], rows3(sq[:, :]), AX, ALU.add).then_inc(var_ready, 1)
                        dve.wait_ge(std_ready, c + 1)
                        ch.link(nc.vector.reciprocal(rstd[:, :], std[:, :]))
                        if not first:
                            dve.wait_ge(sent[q], i * (16 * C))
                        if keep:
                            ch.link(nc.vector.tensor_tensor(rows3(cols(own, c, D)), rows3(t[:, :]), spread(rstd[:, :]), ALU.mult))
                            ch.link(copy(nc, slots[q][:, 0:CD], cols(own, c, D)))
                        else:
                            ch.link(nc.vector.tensor_tensor(rows3(slots[q][:, 0:CD]), rows3(t[:, :]), spread(rstd[:, :]), ALU.mult))
                        nc.vector.tensor_copy(islots[q][:, 0:C], cols(sidx, c)).then_inc(filled, 1)
                        dve.wait_ge(filled, c + 1)

                    per = 2 * (8 + (rowscale is not None) + (sum_scale is not None) + keep)
                    chunk(0, 0, True)
                    chunk(0, 1, True)
                    with ch.loop(1, HALF, per) as i:
                        chunk(i, 0)
                        chunk(i, 1)

                if extra is not None:
                    extra(block, ctx)

        with ExitStack() as ctx:
            keyf, prevf, nextf, tmp = (sb(ctx, n, [P, J]) for n in ("keyf", "prevf", "nextf", "tmp0"))
            prevD, nextD, posi = (sb(ctx, n, [P, J], I32) for n in ("prevD", "nextD", "posi"))
            fill = sb(ctx, "fill", [P, 784 * 2])
            minus = sb(ctx, "minus", [1, D])
            zero = sb(ctx, "zero", [1, D])
            arep = sb(ctx, "arep", [P, D])
            pst = ps(ctx, "pst0", [P, P])
            loaded, stored, made, step0, arep_ready, at_ready = (sem(ctx, n) for n in (
                "loaded0", "stored0", "made0", "dve_0", "arep0", "at0"))
            with nc.Block() as block:
                @block.sync
                def _(sp):
                    for d_, s_ in ((srcD, src_pe), (dstD, dst_pe), (prevD, dst_prev), (nextD, dst_next), (vec, vecs)):
                        sp.dma_start(d_[:, :], s_).then_inc(loaded, 16)
                    sp.wait_ge(step0, 4)
                    sp.dma_start(NT.rearrange("(p n) t -> p (n t)", p=P), fill[:, :]).then_inc(stored, 16)
                    sp.dma_start(U[EP:EP + 1, :], zero[:, :]).then_inc(stored, 16)
                    ends = sorted_src.rearrange("(a n) -> a n", a=1)
                    sp.dma_start(ends[:, 0:1], minus[:, 0:1]).then_inc(stored, 16)
                    sp.dma_start(ends[:, EP + 1:EP + 2], minus[:, 0:1]).then_inc(stored, 16)
                    sp.wait_ge(stored, 64)

                @block.gpsimd
                def _(pool):
                    nc.gpsimd.memset(ident[:, :], 0.0).then_inc(made, 1)
                    nc.gpsimd.memset(ones[:, :], 1.0).then_inc(made, 1)
                    pool.wait_ge(made, 2)
                    nc.gpsimd.affine_select(out=ident[:, :], in_=ident[:, :], compare_op=ALU.not_equal, fill=1.0,
                                            base=0, pattern=[[-1, P]], channel_multiplier=1).then_inc(made, 1)
                    nc.gpsimd.iota(posi[:, :], pattern=[[1, J]], base=0, channel_multiplier=J).then_inc(made, 1)
                    nc.gpsimd.memset(slots[0][:, :], 1.0).then_inc(made, 1)
                    nc.gpsimd.memset(slots[1][:, :], 1.0).then_inc(made, 1)

                @block.vector
                def _(dve):
                    ch = Chain(dve, step0)
                    ch.link(nc.vector.memset(fill[:, 1:784 * 2:2], 1.0))
                    ch.link(nc.vector.memset(fill[:, 0:784 * 2:2], float(EP)))
                    ch.link(nc.vector.memset(minus[:, :], -1.0))
                    ch.link(nc.vector.memset(zero[:, :], 0.0))
                    dve.wait_ge(loaded, 80)
                    ch.link(nc.vector.tensor_copy(keyf[:, :], dstD[:, :]))
                    ch.link(nc.vector.tensor_copy(prevf[:, :], prevD[:, :]))
                    ch.link(nc.vector.tensor_copy(nextf[:, :], nextD[:, :]))
                    dve.wait_ge(made, 6)
                    ch.link(nc.vector.tensor_copy(pos[:, :], posi[:, :]))
                    flags_dve(ch, keyf[:, :], prevf[:, :], nextf[:, :], contD, nendD, FD, sidxD, tmp)
                    nc.vector.tensor_copy(arep[:, :], FD[:, J - 1:J].broadcast_to([P, D])).then_inc(arep_ready, 1)
                    dve.wait_ge(at_ready, 1)
                    ch.link(nc.vector.tensor_copy(ATD[:, :], pst[0:D, :]))

                @block.tensor
                def _(pe):
                    pe.wait_ge(made, 6)
                    pe.wait_ge(arep_ready, 1)
                    nc.tensor.transpose(pst[0:D, :], arep[:, :], ident[:, :]).then_inc(at_ready, 1)

        scal = ExitStack()
        nrm_s, nrm_d, dot = (sb(scal, n, [P, J]) for n in ("nrm_s", "nrm_d", "dot"))
        with ExitStack() as ctx:
            K, V = ([R3[:, (2 * n + b) * SORTW:(2 * n + b + 1) * SORTW] for b in range(2)] for n in range(2))
            above, diff = (R3[:, 4 * SORTW + n * (SORTW // 2):4 * SORTW + (n + 1) * (SORTW // 2)] for n in range(2))
            sign = R3[:, 5 * SORTW:6 * SORTW]
            place, bits = (R3[:, n * SORTW:(n + 1) * SORTW].bitcast(I32) for n in (6, 7))
            prod = sb(ctx, "prod1", [P, CD])
            eps1 = sb(ctx, "eps1", [P, 1])
            kT, vT = ps(ctx, "kT", [P, SORTW]), ps(ctx, "vT", [P, SORTW])
            taken, kept, placed, turn, turned, sorted_, stored, step1 = (sem(ctx, n) for n in (
                "taken1", "kept1", "placed1", "turn1", "turned1", "sorted1", "stored1", "dve_1"))
            staged = [sem(ctx, f"staged{q}_1") for q in range(2)]
            copied = [sem(ctx, f"copied{q}_1") for q in range(2)]
            got = [sem(ctx, f"got{q}_1") for q in range(2)]
            with dense_buffers(ctx, "t1") as (din, dout, tmp, small, ds_), nc.Block() as block:
                @block.gpsimd
                def _(pool):
                    nc.gpsimd.iota(place[:, :], pattern=[[1, SORTW]], base=0, channel_multiplier=SORTW).then_inc(placed, 1)
                    gather_pass(pool, staged, got, (x, x), D, MAXROW)

                @block.sync
                def _(sp):
                    def indices(c, q):
                        sp.dma_start(islots[q][:, 0:C], cols(srcD, c)).then_inc(staged[q], 16)
                        sp.dma_start(islots[q][:, C:2 * C], cols(dstD, c)).then_inc(staged[q], 16)

                    def keep(i, q):
                        c = i * 2 + q
                        sp.wait_ge(got[q], i * (32 * C) + 32 * C)
                        both = slots[q][:, :].rearrange("p (j t f) -> p j t f", t=2, f=D)
                        sp.dma_start(rows3(cols(R1, c, D)), both[:, :, 0, :]).then_inc(copied[q], 16)
                        sp.dma_start(rows3(cols(R2, c, D)), both[:, :, 1, :]).then_inc(copied[q], 16)
                        sp.wait_ge(copied[q], i * 32 + 32)

                    indices(0, 0)
                    indices(1, 1)
                    with sp.Fori(0, HALF - 1) as i:
                        for q in range(2):
                            keep(i, q)
                            indices(i * 2 + q + 2, q)
                    keep(HALF - 1, 0)
                    keep(HALF - 1, 1)
                    sp.wait_ge(sorted_, 1)
                    sp.dma_start(sorted_src[1:EP + 1].rearrange("(p n) -> p n", p=SORTP), K[0][0:SORTP, :]).then_inc(stored, 16)
                    sp.dma_start(sorted_dst.rearrange("(p n) -> p n", p=SORTP), V[0][0:SORTP, :]).then_inc(stored, 16)
                    sp.wait_ge(stored, 32)

                @block.scalar
                def _(act):
                    act.wait_ge(step1, 1)
                    dense_act(act, eps1, x, T1, ds_, din, dout, tmp)

                @block.tensor
                def _(pe):
                    for n in range(2 * (LOG - 9)):
                        pe.wait_ge(turn, n + 1)
                        for q in range(4):
                            b = slice(q * P, (q + 1) * P)
                            nc.tensor.transpose(kT[:, b], K[0][:, b], ident[:, :])
                            last = nc.tensor.transpose(vT[:, b], V[0][:, b], ident[:, :])
                        last.then_inc(turned, 1)

                @block.vector
                def _(dve):
                    ch = Chain(dve, step1)
                    ch.link(nc.vector.memset(eps1[:, :], LNEPS))
                    dense_dve(dve, ch, ds_, din, dout, tmp, small)
                    for b, t in ((K, srcD), (V, dstD)):
                        ch.link(nc.vector.memset(b[0][:, J:SORTW], float(N)))
                        ch.link(nc.vector.tensor_copy(b[0][:, 0:J], t[:, :]))
                    dve.wait_ge(placed, 1)
                    ch.link(nc.vector.tensor_single_scalar(bits[:, :], place[:, :], 1, ALU.logical_shift_right))
                    ch.link(nc.vector.tensor_tensor(place[:, :], place[:, :], bits[:, :], ALU.bitwise_xor))
                    ch.link(nc.vector.tensor_single_scalar(bits[:, :], bits[:, :], 1, ALU.bitwise_and))
                    turns = [0]
                    now = [0]

                    def transpose():
                        if now[0] == 1:
                            ch.link(nc.vector.tensor_copy(K[0][:, :], K[1][:, :]))
                            ch.link(nc.vector.tensor_copy(V[0][:, :], V[1][:, :]))
                            now[0] = 0
                        dve.sem_inc(turn, 1)
                        turns[0] += 1
                        dve.wait_ge(turned, turns[0])
                        ch.tick(nc.vector.tensor_copy(K[0][:, :], kT[:, :]))
                        ch.link(nc.vector.tensor_copy(V[0][:, :], vT[:, :]))

                    def compare(stride):
                        a, b = now[0], 1 - now[0]
                        kk, vv, kn, vn = (t[:, :].rearrange("p (n t s) -> p n t s", t=2, s=stride)
                                          for t in (K[a], V[a], K[b], V[b]))
                        ab, df = (t[:, :].rearrange("p (n s) -> p n s", s=stride) for t in (above, diff))
                        ch.tick(nc.vector.tensor_tensor(df, vv[:, :, 1], vv[:, :, 0], ALU.subtract))
                        ch.tick(nc.vector.tensor_tensor(ab, kk[:, :, 0], kk[:, :, 1], ALU.is_gt))
                        ch.tick(nc.vector.tensor_tensor(kn[:, :, 0], kk[:, :, 0], kk[:, :, 1], ALU.min))
                        ch.link(nc.vector.tensor_tensor(kn[:, :, 1], kk[:, :, 0], kk[:, :, 1], ALU.max))
                        ch.link(nc.vector.tensor_tensor(df, df, ab, ALU.mult))
                        ch.tick(nc.vector.tensor_tensor(vn[:, :, 0], vv[:, :, 0], df, ALU.add))
                        ch.link(nc.vector.tensor_tensor(vn[:, :, 1], vv[:, :, 1], df, ALU.subtract))
                        now[0] = b

                    for k in range(1, LOG + 1):
                        if k > 1:
                            ch.link(nc.vector.tensor_scalar(bits[:, :], place[:, :], k - 1, 1,
                                                            ALU.logical_shift_right, ALU.bitwise_and))
                        ch.link(nc.vector.tensor_scalar(sign[:, :], bits[:, :], -2.0, 1.0, ALU.mult, ALU.add))
                        ch.link(nc.vector.tensor_tensor(K[now[0]][:, :], K[now[0]][:, :], sign[:, :], ALU.mult))
                        if k > 9:
                            transpose()
                            for b in range(k - 1, 8, -1):
                                compare(1 << (b - 9))
                            transpose()
                        for b in range(min(k, 9) - 1, -1, -1):
                            compare(1 << b)
                    if now[0] == 1:
                        ch.link(nc.vector.tensor_copy(K[0][:, :], K[1][:, :]))
                        ch.link(nc.vector.tensor_copy(V[0][:, :], V[1][:, :]))
                    dve.sem_inc(sorted_, 1)

                    with ch.loop(0, HALF, 12) as i:
                        for q in range(2):
                            c = i * 2 + q
                            dve.wait_ge(copied[q], i * 32 + 32)
                            for a, b, o in ((R1, R1, nrm_s), (R2, R2, nrm_d), (R1, R2, dot)):
                                ch.link(nc.vector.tensor_tensor(prod[:, :], cols(a, c, D), cols(b, c, D), ALU.mult))
                                ch.link(nc.vector.tensor_reduce(cols(o, c), rows3(prod[:, :]), AX, ALU.add))

        with ExitStack() as ctx:
            e_, m_, mask_, t_ = (sb(ctx, n, [P, J]) for n in ("e2", "m2", "mask2", "t2"))
            ccol = sb(ctx, "ccol", [P, 1])
            brow = sb(ctx, "brow", [P, 1])
            AB, AM = sb(ctx, "AB", [1, P]), sb(ctx, "AM", [1, P])
            pst, psb = ps(ctx, "pst2", [P, P]), ps(ctx, "psb2", [P, D])
            cs = chain_sems(ctx, "2")
            last_ready = cs[0]
            step2, rooted, expd, asked = (sem(ctx, n) for n in ("dve_2", "rooted2", "exp2", "asked2"))
            with nc.Block() as block:
                @block.scalar
                def _(act):
                    act.wait_ge(asked, 1)
                    nc.scalar.activation(nrm_s[:, :], nrm_s[:, :], ACT.Sqrt).then_inc(rooted, 1)
                    nc.scalar.activation(nrm_d[:, :], nrm_d[:, :], ACT.Sqrt).then_inc(rooted, 1)
                    act.wait_ge(asked, 2)
                    nc.scalar.activation(dot[:, :], e_[:, :], ACT.Exp).then_inc(expd, 1)

                @block.tensor
                def _(pe):
                    pe.wait_ge(last_ready, 1)
                    nc.tensor.transpose(pst[0:1, :], brow[:, :], ident[:, :]).then_inc(cs[1], 1)
                    pe.wait_ge(cs[2], 1)
                    nc.tensor.transpose(psb[:, 0:1], crow[0:1, 0:P], ident[0:1, 0:1]).then_inc(cs[3], 1)
                    carries_pe(pe, cs, 1, 1, m_[:, J - 1:J], pst, psb)
                    carries_pe(pe, cs, 2, 1, t_[:, 0:1], pst, psb, backward=True)
                    carries_pe(pe, cs, 3, 1, t_[:, J - 1:J], pst, psb)
                    carries_pe(pe, cs, 4, D, R3[:, J * D:(J + 1) * D], pst, psb)

                @block.vector
                def _(dve):
                    ch = Chain(dve, step2)
                    v = nc.vector
                    ch.tick(v.tensor_scalar(nrm_s[:, :], nrm_s[:, :], 1e-24, None, ALU.max))
                    ch.link(v.tensor_scalar(nrm_d[:, :], nrm_d[:, :], 1e-24, None, ALU.max))
                    dve.sem_inc(asked, 1)
                    ch.link(v.tensor_tensor_scan(t_[:, J - 1::-1], nendD[:, J - 1::-1], nendD[:, J - 1::-1], 1.0, ALU.mult, ALU.min))
                    ch.link(v.tensor_copy(brow[:, :], t_[:, 0:1]))
                    ch.link(v.memset(crow[:, :], 0.0))
                    dve.sem_inc(last_ready, 1)
                    dve.wait_ge(cs[1], 1)
                    ch.link(v.tensor_copy(AB[:, :], pst[0:1, :]))
                    ch.link(v.tensor_scalar(AM[:, :], ATD[0:1, :], -1.0, BIG, ALU.add, ALU.mult))
                    dve.sem_inc(cs[2], 1)
                    dve.wait_ge(cs[3], 1)
                    ch.link(v.memset(R3[:, 0:D], 0.0))
                    ch.link(v.tensor_scalar(mask_[:, :], contD[:, :], -1.0, BIG, ALU.add, ALU.mult))
                    dve.wait_ge(rooted, 2)
                    ch.link(v.tensor_tensor(nrm_s[:, :], nrm_s[:, :], nrm_d[:, :], ALU.mult))
                    ch.link(v.reciprocal(nrm_s[:, :], nrm_s[:, :]))
                    ch.link(v.tensor_tensor(e_[:, :], dot[:, :], nrm_s[:, :], ALU.mult))
                    ch.link(v.tensor_scalar(e_[:, :], e_[:, :], betav, None, ALU.mult))
                    ch.link(v.tensor_tensor_scan(m_[:, :], mask_[:, :], e_[:, :], -BIG, ALU.add, ALU.max))
                    dve.sem_inc(last_ready, 1)
                    carries_dve(ch, cs, 1, 1, AM, pst, psb, ccol[:, :], ALU.add, ALU.max, -BIG)
                    ch.link(v.tensor_tensor_scan(m_[:, :], mask_[:, :], e_[:, :], ccol[:, :], ALU.add, ALU.max))
                    ch.link(v.tensor_scalar(mask_[:, :], nendD[:, :], -1.0, 1.0, ALU.mult, ALU.add))
                    ch.link(v.tensor_tensor(mask_[:, :], mask_[:, :], m_[:, :], ALU.mult))
                    ch.link(v.tensor_tensor_scan(t_[:, J - 1::-1], nendD[:, J - 1::-1], mask_[:, J - 1::-1], 0.0, ALU.mult, ALU.add))
                    dve.sem_inc(last_ready, 1)
                    carries_dve(ch, cs, 2, 1, AB, pst, psb, ccol[:, :], ALU.mult, ALU.add, 0.0, backward=True)
                    ch.link(v.tensor_tensor_scan(t_[:, J - 1::-1], nendD[:, J - 1::-1], mask_[:, J - 1::-1], ccol[:, :], ALU.mult, ALU.add))
                    ch.link(v.tensor_tensor(e_[:, :], e_[:, :], t_[:, :], ALU.subtract))
                    dve.sem_inc(asked, 1)
                    dve.wait_ge(expd, 1)
                    ch.link(v.tensor_tensor_scan(t_[:, :], contD[:, :], dot[:, :], 0.0, ALU.mult, ALU.add))
                    dve.sem_inc(last_ready, 1)
                    carries_dve(ch, cs, 3, 1, ATD, pst, psb, ccol[:, :], ALU.mult, ALU.add, 0.0)
                    ch.link(v.tensor_tensor_scan(t_[:, :], contD[:, :], dot[:, :], ccol[:, :], ALU.mult, ALU.add))
                    ch.link(v.reciprocal(nrm_d[:, :], t_[:, :]))
                    ch.link(v.tensor_tensor(rows3(R1[:, :]), rows3(R1[:, :]), spread(dot[:, :]), ALU.mult))
                    feature_scan(ch, contD, R1, R3)
                    dve.sem_inc(last_ready, 1)
                    carries_dve(ch, cs, 4, D, ATD, pst, psb, carry[:, :], ALU.mult, ALU.add, 0.0)

        finish("l0", R2, R3, FD, sidxD, T1, rowscale=nrm_d)
        scal.close()

        recycle()
        ordS = ExitStack()
        contS, FS, degrow = (sb(ordS, n, [P, J]) for n in ("contS", "FS", "degrow"))
        valid, posS = sb(ordS, "valid", [P, J]), sb(ordS, "posS", [P, J])
        sidxS, srcS, dstS = (sb(ordS, n, [P, J], I32) for n in ("sidxS", "srcS", "dstS"))
        ATS = sb(ordS, "ATS", [D, P])
        with ExitStack() as ctx:
            keyf, prevf, nextf, tmp, nendS, cnt, t_ = (R3[:, D + n * J:D + (n + 1) * J] for n in range(7))
            ccol, brow = sb(ctx, "ccol4", [P, 1]), sb(ctx, "brow4", [P, 1])
            AB = sb(ctx, "AB4", [1, P])
            arep = sb(ctx, "arep4", [P, D])
            eps1 = sb(ctx, "eps4", [P, 1])
            pst, psb = ps(ctx, "pst4", [P, P]), ps(ctx, "psb4", [P, D])
            cs = chain_sems(ctx, "4")
            last_ready = cs[0]
            step4, loaded, filled = (sem(ctx, n) for n in ("dve_4", "loaded4", "filled4"))
            sent = [sem(ctx, f"sent{q}_4") for q in range(2)]
            with dense_buffers(ctx, "t2") as (din, dout, dtmp, small, ds_), nc.Block() as block:
                @block.sync
                def _(sp):
                    for d_, s_ in ((prevf, sorted_src[0:EP]), (keyf, sorted_src[1:EP + 1]),
                                   (nextf, sorted_src[2:EP + 2]), (tmp, sorted_dst)):
                        sp.dma_start(d_, s_.rearrange("(p n) -> p n", p=P)).then_inc(loaded, 16)

                @block.gpsimd
                def _(pool):
                    scatter_pass(pool, filled, sent, NT, 2)

                @block.scalar
                def _(act):
                    act.wait_ge(step4, 1)
                    dense_act(act, eps1, T1, T2, ds_, din, dout, dtmp)

                @block.tensor
                def _(pe):
                    pe.wait_ge(last_ready, 1)
                    nc.tensor.transpose(pst[0:D, :], arep[:, :], ident[:, :]).then_inc(cs[1], 1)
                    pe.wait_ge(cs[2], 1)
                    nc.tensor.transpose(psb[:, 0:1], crow[0:1, 0:P], ident[0:1, 0:1]).then_inc(cs[3], 1)
                    pe.wait_ge(last_ready, 2)
                    nc.tensor.transpose(pst[0:1, :], brow[:, :], ident[:, :]).then_inc(cs[1], 1)
                    pe.wait_ge(cs[2], 2)
                    nc.tensor.transpose(psb[:, 0:1], crow[0:1, 0:P], ident[0:1, 0:1]).then_inc(cs[3], 1)
                    carries_pe(pe, cs, 2, 1, cnt[:, J - 1:J], pst, psb)
                    carries_pe(pe, cs, 3, 1, t_[:, 0:1], pst, psb, backward=True)

                @block.vector
                def _(dve):
                    v = nc.vector
                    ch = Chain(dve, step4)
                    ch.link(v.memset(eps1[:, :], LNEPS))
                    dve.wait_ge(loaded, 64)
                    ch.link(v.tensor_copy(srcS[:, :], keyf))
                    ch.link(v.tensor_copy(dstS[:, :], tmp))
                    ch.link(v.tensor_scalar(valid[:, :], keyf, float(N), None, ALU.is_lt))
                    flags_dve(ch, keyf, prevf, nextf, contS, nendS, FS, sidxS, tmp)
                    ch.link(v.tensor_copy(arep[:, :], FS[:, J - 1:J].broadcast_to([P, D])))
                    dve.sem_inc(last_ready, 1)
                    dve.wait_ge(cs[1], 1)
                    ch.link(v.tensor_copy(ATS[:, :], pst[0:D, :]))
                    dve.sem_inc(cs[2], 1)
                    dve.wait_ge(cs[3], 1)
                    ch.link(v.tensor_tensor_scan(t_[:, J - 1::-1], nendS[:, J - 1::-1], nendS[:, J - 1::-1], 1.0, ALU.mult, ALU.min))
                    ch.link(v.tensor_copy(brow[:, :], t_[:, 0:1]))
                    dve.sem_inc(last_ready, 1)
                    dve.wait_ge(cs[1], 2)
                    ch.link(v.tensor_copy(AB[:, :], pst[0:1, :]))
                    dve.sem_inc(cs[2], 1)
                    dve.wait_ge(cs[3], 2)
                    ch.link(v.tensor_tensor_scan(cnt, contS[:, :], valid[:, :], 0.0, ALU.mult, ALU.add))
                    dve.sem_inc(last_ready, 1)
                    carries_dve(ch, cs, 2, 1, ATS, pst, psb, ccol[:, :], ALU.mult, ALU.add, 0.0)
                    ch.link(v.tensor_tensor_scan(cnt, contS[:, :], valid[:, :], ccol[:, :], ALU.mult, ALU.add))
                    ch.link(v.tensor_scalar(tmp, nendS, -1.0, 1.0, ALU.mult, ALU.add))
                    ch.link(v.tensor_tensor(tmp, tmp, cnt, ALU.mult))
                    ch.link(v.tensor_tensor_scan(t_[:, J - 1::-1], nendS[:, J - 1::-1], tmp[:, J - 1::-1], 0.0, ALU.mult, ALU.add))
                    dve.sem_inc(last_ready, 1)
                    carries_dve(ch, cs, 3, 1, AB, pst, psb, ccol[:, :], ALU.mult, ALU.add, 0.0, backward=True)
                    ch.link(v.tensor_tensor_scan(degrow[:, J - 1::-1], nendS[:, J - 1::-1], tmp[:, J - 1::-1], ccol[:, :], ALU.mult, ALU.add))

                    def chunk(i, q, first=False):
                        c = i * 2 + q
                        if not first:
                            dve.wait_ge(sent[q], i * (16 * C))
                        row = slots[q][:, 0:2 * C].rearrange("p (j t) -> p j t", t=2)
                        ch.tick(copy(nc, row[:, :, 0], cols(pos, c)))
                        ch.tick(v.tensor_copy(row[:, :, 1], cols(degrow, c)))
                        v.tensor_copy(islots[q][:, 0:C], cols(sidxS, c)).then_inc(filled, 1)

                    chunk(0, 0, True)
                    chunk(0, 1, True)
                    dense_dve(dve, ch, ds_, din, dout, dtmp, small)
                    with ch.loop(1, HALF, 4) as i:
                        chunk(i, 0)
                        chunk(i, 1)

        bn = ExitStack()
        W1bd, W2bd = sb(bn, "W1bd", [P, 2 * D]), sb(bn, "W2bd", [P, P])
        tT = sb(bn, "tT", [P, (C // 2) * P])
        psT = ps(bn, "psT", [P, 4 * 512])
        psH = ps(bn, "psH", [P, 2 * 512])
        with ExitStack() as ctx:
            taken, step5, wz, wl, flipped, tcopied, multiplied, used = (sem(ctx, n) for n in (
                "taken5", "dve_5", "wz5", "wl5", "flipped5", "tcopied5", "mult5", "used5"))
            staged = [sem(ctx, f"staged{q}_5") for q in range(2)]
            got = [sem(ctx, f"got{q}_5") for q in range(2)]
            with nc.Block() as block:
                @block.gpsimd
                def _(pool):
                    gather_pass(pool, staged, got, (T1, T1), D, MAXROW)

                @block.sync
                def _(sp):
                    sp.wait_ge(wz, 2)
                    for a in range(2):
                        sp.dma_start(W1bd[a * 2 * D:(a + 1) * 2 * D, a * D:(a + 1) * D], W1).then_inc(wl, 16)
                    for a in range(4):
                        sp.dma_start(W2bd[a * D:(a + 1) * D, a * D:(a + 1) * D], W2).then_inc(wl, 16)
                    stage_indices(sp, taken, staged, (srcS, dstS))

                @block.tensor
                def _(pe):
                    pe.wait_ge(wl, 16 * 6)
                    with pe.Fori(0, HALF) as i:
                        for q in range(2):
                            c = i * 2 + q
                            pe.wait_ge(got[q], i * (32 * C) + 32 * C)
                            pe.wait_ge(tcopied, c + 1)
                            for m in range(C // 2):
                                last = nc.tensor.transpose(psT[:, m * P:(m + 1) * P], slots[q][:, m * P:(m + 1) * P], ident[:, :])
                            last.then_inc(flipped, 1)
                            pe.wait_ge(tcopied, c + 2)
                            pe.wait_ge(used, c + 1)
                            for m in range(C // 2):
                                last = nc.tensor.matmul(psH[:, m * 2 * D:(m + 1) * 2 * D], tT[:, m * P:(m + 1) * P],
                                                        W1bd[:, :], start=True, stop=True)
                            last.then_inc(multiplied, 1)

                @block.scalar
                def _(act):
                    act.sem_inc(tcopied, 1)
                    with act.Fori(0, NCH) as c:
                        act.wait_ge(flipped, c + 1)
                        act.wait_ge(multiplied, c + 0) if False else None
                        nc.scalar.activation(tT[:, :], psT[:, 0:(C // 2) * P], ACT.Copy).then_inc(tcopied, 1)

                @block.vector
                def _(dve):
                    v = nc.vector
                    ch = Chain(dve, step5)
                    v.memset(W1bd[:, :], 0.0).then_inc(wz, 1)
                    v.memset(W2bd[:, :], 0.0).then_inc(wz, 1)
                    dve.sem_inc(taken, 2)
                    dve.sem_inc(used, 1)
                    with ch.loop(0, HALF, 4) as i:
                        for q in range(2):
                            c = i * 2 + q
                            dve.wait_ge(got[q], i * (32 * C) + 32 * C)
                            both = slots[q][:, :].rearrange("p (j t f) -> p j t f", t=2, f=D)
                            ch.link(copy(nc, rows3(cols(R2, c, D)), both[:, :, 0, :]))
                            dve.wait_ge(multiplied, c + 1)
                            h = rows3(cols(R1, c, D))
                            ch.link(v.tensor_tensor(h, rows3(psH[:, 0:CD]), repeat(b1v, C), ALU.add))
                            v.tensor_tensor(h, h, spread(cols(valid, c)), ALU.mult).then_inc(used, 1)
                            dve.sem_inc(taken, 1)

        with ExitStack() as ctx:
            part = sb(ctx, "part6", [P, D])
            mean, gm, vr = (sb(ctx, n, [P, D]) for n in ("mean6", "gm6", "vr6"))
            hn = sb(ctx, "hn6", [P, CD])
            eps6 = sb(ctx, "eps6", [P, 1])
            pss = [ps(ctx, "pssum", [P, D])]
            pst = ps(ctx, "pst6", [P, P])
            psb = pst
            cs = chain_sems(ctx, "6")
            step6, summed, total, rooted, asked, relued, flipped, tcopied, multiplied, hready = (sem(ctx, n) for n in (
                "dve_6", "summed6", "total6", "rooted6", "asked6", "relued6", "flipped6", "tcopied6", "mult6", "hready6"))
            NG = C // 4
            with nc.Block() as block:
                @block.tensor
                def _(pe):
                    def totals(n):
                        pe.wait_ge(summed, n + 1)
                        nc.tensor.matmul(pss[0][:, :], ones[:, :], part[:, :], start=True, stop=True).then_inc(total, 1)
                    totals(0)
                    totals(1)
                    with pe.Fori(0, NCH) as c:
                        pe.wait_ge(relued, c + 1)
                        for m in range(NG):
                            last = nc.tensor.transpose(psT[:, m * P:(m + 1) * P], hn[:, m * P:(m + 1) * P], ident[:, :])
                        last.then_inc(flipped, 1)
                        pe.wait_ge(tcopied, c + 1)
                        for m in range(NG):
                            last = nc.tensor.matmul(psH[:, m * P:(m + 1) * P], tT[:, m * P:(m + 1) * P], W2bd[:, :],
                                                    start=True, stop=True)
                        last.then_inc(multiplied, 1)
                    totals(2)
                    totals(3)
                    carries_pe(pe, cs, 0, D, R3[:, J * D:(J + 1) * D], pst, psb)

                @block.scalar
                def _(act):
                    act.wait_ge(asked, 1)
                    nc.scalar.activation(vr[:, :], vr[:, :], ACT.Sqrt, bias=eps6[:, :], scale=1.0 / E).then_inc(rooted, 1)
                    with act.Fori(0, NCH) as c:
                        act.wait_ge(hready, c + 1)
                        nc.scalar.activation(hn[:, :], hn[:, :], ACT.Relu).then_inc(relued, 1)
                        act.wait_ge(flipped, c + 1)
                        nc.scalar.activation(tT[:, 0:NG * P], psT[:, 0:NG * P], ACT.Copy).then_inc(tcopied, 1)
                    act.wait_ge(asked, 2)
                    nc.scalar.activation(vr[:, :], vr[:, :], ACT.Sqrt, bias=eps6[:, :], scale=1.0 / E).then_inc(rooted, 1)

                @block.vector
                def _(dve):
                    v = nc.vector
                    ch = Chain(dve, step6)
                    ch.link(v.memset(eps6[:, :], BNEPS))
                    byfeature = R1[:, :].rearrange("p (j f) -> p f j", f=D)
                    R3b = R3[:, D:(J + 1) * D]

                    def stats(n, g):
                        ch.link(v.tensor_reduce(part[:, :], byfeature, AX, ALU.add))
                        dve.sem_inc(summed, 1)
                        dve.wait_ge(total, 2 * n + 1)
                        ch.link(v.tensor_scalar(mean[:, :], pss[0][:, :], 1.0 / E, None, ALU.mult))
                        ch.link(v.tensor_tensor(rows3(R1[:, :]), rows3(R1[:, :]), repeat(mean[:, :], J), ALU.subtract))
                        ch.link(v.tensor_tensor(rows3(R1[:, :]), rows3(R1[:, :]), spread(valid[:, :]), ALU.mult))
                        ch.link(v.tensor_tensor(R3b, R1[:, :], R1[:, :], ALU.mult))
                        ch.link(v.tensor_reduce(part[:, :], R3b.rearrange("p (j f) -> p f j", f=D), AX, ALU.add))
                        dve.sem_inc(summed, 1)
                        dve.wait_ge(total, 2 * n + 2)
                        ch.link(v.tensor_copy(vr[:, :], pss[0][:, :]))
                        dve.sem_inc(asked, 1)
                        dve.wait_ge(rooted, n + 1)
                        ch.link(v.reciprocal(gm[:, :], vr[:, :]))
                        ch.link(v.tensor_tensor(gm[:, :], gm[:, :], g, ALU.mult))

                    stats(0, g1v)
                    with ch.loop(0, NCH, 2) as c:
                        h = rows3(cols(R1, c, D))
                        ch.link(v.tensor_tensor(rows3(hn[:, :]), h, repeat(gm[:, :], C), ALU.mult))
                        v.tensor_tensor(rows3(hn[:, :]), rows3(hn[:, :]), repeat(be1v, C), ALU.add).then_inc(hready, 1)
                        dve.wait_ge(multiplied, c + 1)
                        ch.link(v.tensor_tensor(h, rows3(psH[:, 0:CD]), repeat(b2v, C), ALU.add))
                    ch.link(v.tensor_tensor(rows3(R1[:, :]), rows3(R1[:, :]), spread(valid[:, :]), ALU.mult))
                    stats(1, g2v)
                    ch.link(v.tensor_tensor(rows3(R1[:, :]), rows3(R1[:, :]), repeat(gm[:, :], J), ALU.mult))
                    ch.link(v.tensor_tensor(rows3(R1[:, :]), rows3(R1[:, :]), repeat(be2v, J), ALU.add))
                    ch.link(v.tensor_scalar(R1[:, :], R1[:, :], 0.0, None, ALU.max))
                    feature_scan(ch, contS, R1, R3)
                    dve.sem_inc(cs[0], 1)
                    carries_dve(ch, cs, 0, D, ATS, pst, psb, carry[:, :], ALU.mult, ALU.add, 0.0)
        bn.close()

        finish("l1", R2, R3, FS, sidxS, T2, keep=True)

        recycle()
        wS = valid
        ipos = srcS
        with ExitStack() as ctx:
            pd, dd = (sb(ctx, n, [P, J]) for n in ("pd8", "dd8"))
            eps1 = sb(ctx, "eps8", [P, 1])
            taken, step8, asked, rooted = (sem(ctx, n) for n in ("taken8", "dve_8", "asked8", "rooted8"))
            staged = [sem(ctx, f"staged{q}_8") for q in range(2)]
            got = [sem(ctx, f"got{q}_8") for q in range(2)]
            with dense_buffers(ctx, "t3") as (din, dout, dtmp, small, ds_), nc.Block() as block:
                @block.gpsimd
                def _(pool):
                    gather_pass(pool, staged, got, (NT,), 2, MAXROW)

                @block.sync
                def _(sp):
                    stage_indices(sp, taken, staged, (dstS,))

                @block.scalar
                def _(act):
                    act.wait_ge(step8, 1)
                    dense_act(act, eps1, T2, T3, ds_, din, dout, dtmp)
                    act.wait_ge(asked, 1)
                    nc.scalar.activation(dd[:, :], dd[:, :], ACT.Sqrt).then_inc(rooted, 1)

                @block.vector
                def _(dve):
                    v = nc.vector
                    ch = Chain(dve, step8)
                    ch.link(v.memset(eps1[:, :], LNEPS / (1.0 + ALPHA / GAMMA) ** 2))
                    dve.sem_inc(taken, 2)
                    dense_dve(dve, ch, ds_, din, dout, dtmp, small)
                    with ch.loop(0, HALF, 4) as i:
                        for q in range(2):
                            c = i * 2 + q
                            dve.wait_ge(got[q], i * (16 * C) + 16 * C)
                            row = slots[q][:, 0:2 * C].rearrange("p (j t) -> p j t", t=2)
                            ch.tick(copy(nc, cols(pd, c), row[:, :, 0]))
                            ch.link(v.tensor_copy(cols(dd, c), row[:, :, 1]))
                            dve.sem_inc(taken, 1)
                    ch.link(v.tensor_copy(ipos[:, :], pd[:, :]))
                    ch.link(v.tensor_scalar(degrow[:, :], degrow[:, :], 1.0, None, ALU.max))
                    ch.link(v.tensor_tensor(dd[:, :], dd[:, :], degrow[:, :], ALU.mult))
                    ch.link(v.tensor_scalar(dd[:, :], dd[:, :], 1.0, None, ALU.max))
                    dve.sem_inc(asked, 1)
                    dve.wait_ge(rooted, 1)
                    ch.link(v.reciprocal(dd[:, :], dd[:, :]))
                    ch.link(v.tensor_tensor(wS[:, :], valid[:, :], dd[:, :], ALU.mult))
                    ch.link(v.tensor_scalar(degrow[:, :], wS[:, :], BETA, None, ALU.mult))
        wB = degrow

        def chunk_scan(ch, c, m):
            v = nc.vector
            for f in range(D):
                ch.tick(v.tensor_tensor_scan(
                    R3[:, bass.ds(c * CD + D + f, C, step=D)], cols(contS, c),
                    m[:, f:f + (C - 1) * D + 1:D], R3[:, bass.ds(c * CD + f, 1)], ALU.mult, ALU.add))
            ch.engine.wait_ge(ch.sem, ch.value())

        with ExitStack() as ctx:
            m = sb(ctx, "m9", [P, CD])
            pst, psb = ps(ctx, "pst9", [P, P]), ps(ctx, "psb9", [P, D])
            taken, step9 = sem(ctx, "taken9"), sem(ctx, "dve_9")
            staged = [sem(ctx, f"staged{q}_9") for q in range(2)]
            got = [sem(ctx, f"got{q}_9") for q in range(2)]
            cs = chain_sems(ctx, "9")
            with nc.Block() as block:
                @block.gpsimd
                def _(pool):
                    gather_pass(pool, staged, got, (T2,), D, MAXROW)

                @block.sync
                def _(sp):
                    stage_indices(sp, taken, staged, (dstS,))

                @block.tensor
                def _(pe):
                    carries_pe(pe, cs, 0, D, R3[:, J * D:(J + 1) * D], pst, psb)

                @block.vector
                def _(dve):
                    v = nc.vector
                    ch = Chain(dve, step9)
                    dve.sem_inc(taken, 2)
                    with ch.loop(0, HALF, 68) as i:
                        for q in range(2):
                            c = i * 2 + q
                            dve.wait_ge(got[q], i * (16 * C) + 16 * C)
                            ch.link(v.tensor_tensor(rows3(m[:, :]), rows3(slots[q][:, 0:CD]), spread(cols(wS, c)), ALU.mult))
                            dve.sem_inc(taken, 1)
                            ch.link(v.tensor_scalar(cols(R1, c, D), m[:, :], ALPHA, None, ALU.mult))
                            chunk_scan(ch, c, m)
                    dve.sem_inc(cs[0], 1)
                    carries_dve(ch, cs, 0, D, ATS, pst, psb, carry[:, :], ALU.mult, ALU.add, 0.0)

        with ExitStack() as ctx:
            m = sb(ctx, "m10", [P, CD])
            pst, psb = ps(ctx, "pst10", [P, P]), ps(ctx, "psb10", [P, D])
            taken, step10, fixed, stored = (sem(ctx, n + "10") for n in (
                "taken", "dve_", "fixed", "stored"))
            staged = [sem(ctx, f"staged{q}_10") for q in range(2)]
            got = [sem(ctx, f"got{q}_10") for q in range(2)]
            cs = chain_sems(ctx, "10")
            STEPS = KSTEPS - 1
            Uv = U[0:EP, :].rearrange("(p j) f -> p (j f)", p=P)
            with nc.Block() as block:
                @block.gpsimd
                def _(pool):
                    limit = pool.to_reg(EP)
                    with pool.Fori(0, STEPS) as t:
                        pool.wait_ge(stored, t * (16 * NCH) + 16 * NCH)
                        pool.sem_inc(begun, 1)
                        with pool.Fori(0, HALF) as i:
                            for q in range(2):
                                pool.wait_ge(staged[q], t * (16 * HALF) + i * 16 + 16)
                                pool.sem_inc(begun, 1)
                                gather(pool, i, q, got, (U,), D, limit)

                @block.sync
                def _(sp):
                    with sp.Fori(0, STEPS) as t:
                        with sp.Fori(0, NCH) as c:
                            sp.wait_ge(fixed, t * NCH + c + 1)
                            sp.dma_start(Uv[:, bass.ds(c * CD, CD)], R3[:, bass.ds(c * CD + D, CD)]).then_inc(stored, 16)
                        with sp.Fori(0, HALF) as i:
                            for q in range(2):
                                sp.wait_ge(taken, t * NCH + i * 2 + q + 1)
                                sp.dma_start(islots[q][:, 0:C], cols(ipos, i * 2 + q)).then_inc(staged[q], 16)

                @block.tensor
                def _(pe):
                    with pe.Fori(0, STEPS) as t:
                        carries_pe(pe, cs, t, D, R3[:, J * D:(J + 1) * D], pst, psb)

                @block.vector
                def _(dve):
                    v = nc.vector
                    ch = Chain(dve, step10)
                    dve.sem_inc(taken, 2)
                    with ch.loop(0, STEPS, NCH + HALF * 68 + 2) as t:
                        with ch.loop(0, NCH, 1) as c:
                            ch.link(v.tensor_tensor(rows3(m[:, :]), spread(cols(FS, c)), repeat(carry[:, :], C), ALU.mult))
                            s3 = R3[:, bass.ds(c * CD + D, CD)]
                            v.tensor_tensor(s3, s3, m[:, :], ALU.add).then_inc(fixed, 1)
                            dve.wait_ge(fixed, t * NCH + c + 1)
                        with ch.loop(0, HALF, 68) as i:
                            for q in range(2):
                                c = i * 2 + q
                                dve.wait_ge(got[q], t * (16 * C * HALF) + i * (16 * C) + 16 * C)
                                ch.link(v.tensor_tensor(rows3(m[:, :]), rows3(slots[q][:, 0:CD]), spread(cols(wB, c)), ALU.mult))
                                dve.sem_inc(taken, 1)
                                ch.link(v.tensor_tensor(m[:, :], m[:, :], cols(R1, c, D), ALU.add))
                                chunk_scan(ch, c, m)
                        dve.sem_inc(cs[0], 1)
                        carries_dve(ch, cs, t, D, ATS, pst, psb, carry[:, :], ALU.mult, ALU.add, 0.0)

        finish("l2", R2, R3, FS, sidxS, T3, own_scale=1.0 + ALPHA / GAMMA, sum_scale=BETA / GAMMA)
        ordS.close()

        recycle()
        with ExitStack() as ctx:
            eps1 = sb(ctx, "eps12", [P, 1])
            step12 = sem(ctx, "dve_12")
            with dense_buffers(ctx, "o") as (din, dout, dtmp, small, ds_), nc.Block() as block:
                @block.scalar
                def _(act):
                    act.wait_ge(step12, 1)
                    dense_act(act, eps1, T3, out, ds_, din, dout, dtmp)

                @block.vector
                def _(dve):
                    ch = Chain(dve, step12)
                    ch.link(nc.vector.memset(eps1[:, :], LNEPS))
                    dense_dve(dve, ch, ds_, din, dout, dtmp, small)

        lay.close()

        with ExitStack() as ctx:
            r1, wt = sb(ctx, "r1", [P, J * 3]), sb(ctx, "wt", [P, J])
            w1c, w2c = sb(ctx, "w1c", [10, 48]), sb(ctx, "w2c", [48, 512])
            emb, HT = sb(ctx, "emb", [10, C * P]), sb(ctx, "HT", [48, C * P])
            s1, vd, vtmp = (sb(ctx, n, [P, C * 16]) for n in ("s1", "vd", "vtmp"))
            v1 = [sb(ctx, f"v1_{k}", [P, C * 16]) for k in range(3)]
            v1s = sb(ctx, "v1s", [P, C * 48])
            pr = sb(ctx, "pr", [P, 768])
            T48, T64 = sb(ctx, "T48", [P, C * 48]), sb(ctx, "T64", [P, C * 64])
            st, vd2, vtmp2 = (sb(ctx, n, [P, C * 8]) for n in ("st13", "vd2", "vtmp2"))
            vt = sb(ctx, "vt13", [P, C * 24])
            o16, th = sb(ctx, "o16", [P, 2 * C * 8]), sb(ctx, "th", [P, 2 * C * 8])
            n3, n3b = sb(ctx, "n3", [P, J]), sb(ctx, "n3b", [P, J])
            psHT = ps(ctx, "psHT", [P, 512])
            psw = [ps(ctx, f"psw{b}", [P, 512]) for b in range(2)]
            psx = [ps(ctx, f"psx{b}", [P, 512]) for b in range(2)]
            (taken, step13, loaded, asked, rooted, hid, hidd, embl, embf, w1r, w1u, w2r, w2u, sct, tanhed, pz) = (
                sem(ctx, n + "13") for n in ("taken", "dve_", "loaded", "asked", "rooted", "hid", "hidd", "embl",
                                             "embf", "w1r", "w1u", "w2r", "w2u", "sct", "tanhed", "pz"))
            staged = [sem(ctx, f"staged{q}_13") for q in range(2)]
            got = [sem(ctx, f"got{q}_13") for q in range(2)]
            G4 = C // 4
            C1 = float(32.0 ** -0.5 / 4.0)
            C2 = float(16.0 ** -0.5 / 4.0)
            SQRT3 = float(3.0 ** 0.5)
            with nc.Block() as block:
                @block.gpsimd
                def _(pool):
                    gather_pass(pool, staged, got, (T3, T3), D, MAXROW)

                @block.sync
                def _(sp):
                    sp.dma_start(r1[:, :], attr3).then_inc(loaded, 16)
                    sp.dma_start(wt[:, :], weight).then_inc(loaded, 16)
                    sp.wait_ge(pz, 1)
                    sp.dma_start(w1c[:, 0:16], fc1_w1).then_inc(loaded, 16)
                    sp.dma_start(w1c[:, 32:48], fc2_w1).then_inc(loaded, 16)
                    sp.dma_start(w2c[0:16, :], fc1_w2).then_inc(loaded, 16)
                    sp.dma_start(w2c[32:48, 0:384], fc2_w2).then_inc(loaded, 16)
                    with sp.Fori(0, HALF) as i:
                        for q in range(2):
                            c = i * 2 + q
                            sp.wait_ge(taken, c + 1)
                            sp.dma_start(islots[q][:, 0:C], cols(srcD, c)).then_inc(staged[q], 16)
                            sp.dma_start(islots[q][:, C:2 * C], cols(dstD, c)).then_inc(staged[q], 16)
                            sp.wait_ge(embf, c + 1)
                            sp.dma_start(emb[:, :], attr10t[:, bass.ds(c * (C * P), C * P)]).then_inc(embl, 16)

                @block.tensor
                def _(pe):
                    pe.wait_ge(loaded, 96)
                    with pe.Fori(0, NCH) as c:
                        pe.wait_ge(embl, c * 16 + 16)
                        for g in range(G4):
                            pe.wait_ge(hidd, c * G4 + g + 1)
                            nc.tensor.matmul(psHT[0:48, :], w1c[:, :], emb[:, g * 512:(g + 1) * 512],
                                             start=True, stop=True).then_inc(hid, 1)
                        pe.wait_ge(hidd, c * G4 + G4 + 1)
                        for j in range(C):
                            pe.wait_ge(w1u, c * C + j + 1)
                            nc.tensor.matmul(psw[j % 2][:, :], HT[0:16, j * P:(j + 1) * P], w2c[0:16, :],
                                             start=True, stop=True).then_inc(w1r, 1)
                        for j in range(C):
                            pe.wait_ge(w2u, c * C + j + 1)
                            nc.tensor.matmul(psx[j % 2][:, 0:384], HT[32:48, j * P:(j + 1) * P], w2c[32:48, 0:384],
                                             start=True, stop=True).then_inc(w2r, 1)

                @block.scalar
                def _(act):
                    act.wait_ge(asked, 1)
                    nc.scalar.activation(n3[:, :], n3[:, :], ACT.Sqrt).then_inc(rooted, 1)
                    with act.Fori(0, NCH) as c:
                        for g in range(G4):
                            act.wait_ge(hid, c * G4 + g + 1)
                            if g == 0:
                                act.wait_ge(w2r, c * C + 1)
                            if g == 0:
                                nc.scalar.activation(HT[:, 0:512], psHT[0:48, :], ACT.Relu,
                                                     scale=float(10 ** -0.5)).then_inc(hidd, 1)
                            else:
                                nc.scalar.activation(HT[:, g * 512:(g + 1) * 512], psHT[0:48, :], ACT.Relu,
                                                     scale=float(10 ** -0.5)).then_inc(hidd, 1)
                        act.sem_inc(embf, 1)
                        act.wait_ge(sct, c + 1)
                        nc.scalar.activation(th[:, :], o16[:, :], ACT.Tanh).then_inc(tanhed, 1)

                @block.vector
                def _(dve):
                    v = nc.vector
                    ch = Chain(dve, step13)
                    ch.link(v.memset(w2c[:, :], 0.0))
                    v.memset(w1c[:, :], 0.0).then_inc(pz, 1)
                    dve.sem_inc(taken, 2)
                    dve.sem_inc(w1u, 2)
                    dve.sem_inc(w2u, 2)
                    dve.sem_inc(w2r, 1)
                    dve.sem_inc(hidd, 1)
                    dve.sem_inc(embf, 1)
                    dve.wait_ge(loaded, 96)
                    r3 = r1[:, :].rearrange("p (j k) -> p j k", k=3)
                    ch.link(v.tensor_tensor(n3[:, :], r3[:, :, 0], r3[:, :, 0], ALU.mult))
                    for k in (1, 2):
                        ch.link(v.tensor_tensor(n3b[:, :], r3[:, :, k], r3[:, :, k], ALU.mult))
                        ch.link(v.tensor_tensor(n3[:, :], n3[:, :], n3b[:, :], ALU.add))
                    dve.sem_inc(asked, 1)
                    dve.wait_ge(rooted, 1)
                    ch.link(v.reciprocal(n3b[:, :], n3[:, :]))
                    ch.link(v.tensor_tensor(r3, r3, spread(n3b[:, :], 3), ALU.mult))

                    def direction(c, k):
                        return r1[:, bass.ds(c * (3 * C) + k, C, step=3)]

                    def dot_r(c, parts, acc, tmp, n):
                        ch.link(v.tensor_tensor(rows3(acc, n), parts[0], spread(direction(c, 0), n), ALU.mult))
                        for k in (1, 2):
                            ch.link(v.tensor_tensor(rows3(tmp, n), parts[k], spread(direction(c, k), n), ALU.mult))
                            ch.link(v.tensor_tensor(acc, acc, tmp, ALU.add))

                    with ch.loop(0, HALF, 2 * (5 + 5 + 4 * C + 1 + 1 + 6 + 5 + 4 * C + 1 + 2 + 2 + 9)) as i:
                        for q in range(2):
                            c = i * 2 + q
                            dve.wait_ge(got[q], i * (32 * C) + 32 * C)
                            both = slots[q][:, :].rearrange("p (j t f) -> p j t f", t=2, f=D)
                            ch.tick(copy(nc, rows3(cols(R2, c, D)), both[:, :, 1, :]))
                            ch.tick(v.tensor_copy(s1[:, :].rearrange("p (j t u) -> p j t u", t=2, u=8), both[:, :, :, 0:8]))
                            v1v = v1s[:, :].rearrange("p (j k t u) -> p j k t u", k=3, t=2, u=8)
                            for k in range(3):
                                ch.tick(v.tensor_copy(v1v[:, :, k], both[:, :, :, 8 + k:32:3]))
                            dve.wait_ge(ch.sem, ch.value())
                            dve.sem_inc(taken, 1)
                            v1j = v1s[:, :].rearrange("p (j k u) -> p j k u", k=3, u=16)
                            dot_r(c, [v1j[:, :, k] for k in range(3)], vd[:, :], vtmp[:, :], 16)
                            for j in range(C):
                                w = psw[j % 2][:, :].rearrange("p (g u w) -> p g u w", g=4, w=8)
                                p6 = pr[:, :].rearrange("p (g u w) -> p g u w", g=6, w=8)
                                sj = s1[:, j * 16:(j + 1) * 16].rearrange("p (a u b) -> p a u b", a=1, b=1)
                                dj = vd[:, j * 16:(j + 1) * 16].rearrange("p (u b) -> p u b", b=1)
                                vj = v1s[:, j * 48:(j + 1) * 48].rearrange("p (k u b) -> p k u b", k=3, b=1)
                                dve.wait_ge(w1r, c * C + j + 1)
                                ch.tick(v.tensor_tensor(p6[:, 0:3:2], w[:, 0:3:2], sj.broadcast_to([P, 2, 16, 8]), ALU.mult))
                                ch.tick(v.tensor_tensor(p6[:, 1], w[:, 1], dj.broadcast_to([P, 16, 8]), ALU.mult))
                                ch.link(v.tensor_tensor(p6[:, 3:6], w[:, 3:4].broadcast_to([P, 3, 16, 8]),
                                                        vj.broadcast_to([P, 3, 16, 8]), ALU.mult))
                                dve.sem_inc(w1u, 1)
                                ch.link(v.tensor_reduce(T48[:, j * 48:(j + 1) * 48].rearrange("p (g w) -> p g w", g=6),
                                                        p6.rearrange("p g u w -> p g w u"), AX, ALU.add))
                            ch.link(v.tensor_scalar(T48[:, :], T48[:, :], C1, None, ALU.mult))
                            t6 = T48[:, :].rearrange("p (j g w) -> p j g w", g=6, w=8)
                            vt3 = vt[:, :].rearrange("p (j k w) -> p j k w", k=3, w=8)
                            ch.tick(v.tensor_tensor(rows3(st[:, :], 8), t6[:, :, 0], t6[:, :, 1], ALU.add))
                            for k in range(3):
                                ch.link(v.tensor_tensor(rows3(vtmp2[:, :], 8), t6[:, :, 2], spread(direction(c, k), 8), ALU.mult))
                                ch.link(v.scalar_tensor_tensor(vt3[:, :, k], rows3(vtmp2[:, :], 8), SQRT3, t6[:, :, 3 + k], ALU.mult, ALU.add))
                            dot_r(c, [vt3[:, :, k] for k in range(3)], vd2[:, :], vtmp2[:, :], 8)
                            for j in range(C):
                                w = psx[j % 2][:, 0:384].rearrange("p (g u w) -> p g u w", g=6, w=8)
                                p8 = pr[:, 0:512].rearrange("p (g u w) -> p g u w", g=8, w=8)
                                sj = st[:, j * 8:(j + 1) * 8].rearrange("p (a u b) -> p a u b", a=1, b=1)
                                dj = vd2[:, j * 8:(j + 1) * 8].rearrange("p (a u b) -> p a u b", a=1, b=1)
                                vj = vt[:, j * 24:(j + 1) * 24].rearrange("p (k u b) -> p k u b", k=3, b=1)
                                dve.wait_ge(w2r, c * C + j + 2)
                                ch.tick(v.tensor_tensor(p8[:, 0:5:2], w[:, 0:5:2], sj.broadcast_to([P, 3, 8, 8]), ALU.mult))
                                ch.tick(v.tensor_tensor(p8[:, 1:4:2], w[:, 1:4:2], dj.broadcast_to([P, 2, 8, 8]), ALU.mult))
                                ch.link(v.tensor_tensor(p8[:, 5:8], w[:, 5:6].broadcast_to([P, 3, 8, 8]),
                                                        vj.broadcast_to([P, 3, 8, 8]), ALU.mult))
                                dve.sem_inc(w2u, 1)
                                ch.link(v.tensor_reduce(T64[:, j * 64:(j + 1) * 64].rearrange("p (g w) -> p g w", g=8),
                                                        p8.rearrange("p g u w -> p g w u"), AX, ALU.add))
                            ch.link(v.tensor_scalar(T64[:, :], T64[:, :], C2, None, ALU.mult))
                            t8 = T64[:, :].rearrange("p (j g w) -> p j g w", g=8, w=8)
                            oo = o16[:, :].rearrange("p (a j w) -> p a j w", a=2, w=8)
                            ch.tick(v.tensor_tensor(oo[:, 0], t8[:, :, 0], t8[:, :, 1], ALU.add))
                            ch.link(v.tensor_tensor(oo[:, 1], t8[:, :, 2], t8[:, :, 3], ALU.add))
                            dve.sem_inc(sct, 1)
                            dve.wait_ge(tanhed, c + 1)
                            tt = th[:, :].rearrange("p (a j w) -> p a j w", a=2, w=8)
                            eo = rows3(cols(R1, c, D))
                            wj = cols(wt, c)
                            ch.tick(v.tensor_tensor(eo[:, :, 0:8], tt[:, 0], spread(wj, 8), ALU.mult))
                            ch.link(v.tensor_tensor(tt[:, 1], tt[:, 1], spread(wj, 8), ALU.mult))
                            for k in range(3):
                                ch.link(v.tensor_tensor(rows3(vtmp2[:, :], 8), t8[:, :, 4], spread(direction(c, k), 8), ALU.mult))
                                ch.link(v.scalar_tensor_tensor(rows3(vtmp2[:, :], 8), rows3(vtmp2[:, :], 8), SQRT3, t8[:, :, 5 + k], ALU.mult, ALU.add))
                                ch.link(v.tensor_tensor(eo[:, :, 8 + k:32:3], rows3(vtmp2[:, :], 8), tt[:, 1], ALU.mult))

        lay2 = ExitStack()
        R3 = sb(lay2, "R3b", [P, (J + 1) * D])
        with ExitStack() as ctx:
            pst, psb = ps(ctx, "pst14", [P, P]), ps(ctx, "psb14", [P, D])
            cs = chain_sems(ctx, "14")
            step14 = sem(ctx, "dve_14")
            with nc.Block() as block:
                @block.tensor
                def _(pe):
                    carries_pe(pe, cs, 0, D, R3[:, J * D:(J + 1) * D], pst, psb)

                @block.vector
                def _(dve):
                    ch = Chain(dve, step14)
                    feature_scan(ch, contD, R1, R3)
                    dve.sem_inc(cs[0], 1)
                    carries_dve(ch, cs, 0, D, ATD, pst, psb, carry[:, :], ALU.mult, ALU.add, 0.0)

        finish("l3", R2, R3, FD, sidxD, out)
        lay2.close()


def kernel(x, src, dst, edge_attr_10, edge_attr_3, edge_weight, L0_gnn_beta, L1_gnn_W1, L1_gnn_b1,
           L1_gnn_gamma1, L1_gnn_beta1, L1_gnn_W2, L1_gnn_b2, L1_gnn_gamma2, L1_gnn_beta2,
           L3_gnn_fc1_w1, L3_gnn_fc1_w2, L3_gnn_fc2_w1, L3_gnn_fc2_w2):
    import concourse.bacc as bacc
    from concourse.bass_utils import run_bass_kernel_spmd

    def edges(a, fill, shift=0):
        a = np.asarray(a)
        out = np.full((EP + 2,) + a.shape[1:], fill, a.dtype)
        out[0] = out[EP + 1] = -1 if shift else fill
        out[1:E + 1] = a
        return np.ascontiguousarray(out[1 + shift:1 + shift + EP].reshape((P, J) + a.shape[1:]))

    def row(a, n):
        return np.broadcast_to(np.resize(np.asarray(a), (1, n)), (P, n))

    arrays = {
        "x": np.asarray(x),
        "src": edges(src, N), "dst": edges(dst, N), "dst_prev": edges(dst, N, -1), "dst_next": edges(dst, N, 1),
        "attr3": edges(edge_attr_3, 1).reshape(P, J * 3),
        "attr10t": np.ascontiguousarray(edges(edge_attr_10, 0).transpose(2, 1, 0).reshape(10, J * P)),
        "weight": edges(edge_weight, 0),
        "W1": np.asarray(L1_gnn_W1), "W2": np.asarray(L1_gnn_W2),
        "vecs": np.ascontiguousarray(np.concatenate(
            [row(a, D) for a in (L1_gnn_b1, L1_gnn_gamma1, L1_gnn_beta1, L1_gnn_b2, L1_gnn_gamma2, L1_gnn_beta2,
                                 L0_gnn_beta)], axis=1)),
        "fc1_w1": np.asarray(L3_gnn_fc1_w1), "fc1_w2": np.asarray(L3_gnn_fc1_w2),
        "fc2_w1": np.asarray(L3_gnn_fc2_w1), "fc2_w2": np.asarray(L3_gnn_fc2_w2),
    }
    nc = bacc.Bacc("TRN2", target_bir_lowering=False, num_devices=1)
    t = {k: nc.dram_tensor("in_" + k, a.shape, mybir.dt.from_np(a.dtype), kind="ExternalInput").ap()
         for k, a in arrays.items()}
    out = nc.dram_tensor("out_rows", (N, D), F32, kind="ExternalOutput").ap()
    build(nc, t["x"], t["src"], t["dst"], t["dst_prev"], t["dst_next"], t["attr3"], t["attr10t"], t["weight"],
          None, t["W1"], t["W2"], t["vecs"], t["fc1_w1"], t["fc1_w2"], t["fc2_w1"], t["fc2_w2"], out)
    r = run_bass_kernel_spmd(nc, [{"in_" + k: a for k, a in arrays.items()}], core_ids=[0])
    return r.results[0]["out_rows"]
```

```python
import numpy as np
import concourse.bass as bass
from concourse import mybir
from concourse.alu_op_type import AluOpType as ALU
from contextlib import ExitStack, contextmanager

F32 = mybir.dt.float32
I32 = mybir.dt.int32
ACT = mybir.ActivationFunctionType
AX = mybir.AxisListType.X

P = 128
N = 100000
E = 50000
D = 32
J = 392
EP = P * J
C = 28
NCH = J // C
HALF = NCH // 2
CD = C * D
SORTW = 512
SORTP = EP // SORTW
LOG = 16
R = 32
NODES_CH = P * R
DENSE = N // NODES_CH
TAILP = (N - DENSE * NODES_CH) // R
LNEPS = 1e-5
BNEPS = 1e-5
BIG = 3.0e38
KSTEPS = 10
UW = D + 1
ALPHA, BETA = 0.1, 0.9
GAMMA = BETA ** KSTEPS + ALPHA * sum(BETA ** i for i in range(KSTEPS))
MAXROW = N - 1


class Chain:

    def __init__(self, engine, sem):
        self.engine, self.sem, self.k, self.terms, self.written = engine, sem, 0, [], 0

    def value(self):
        v = self.k
        for i, start, per in self.terms:
            v = (i - start if start else i) * per + v
        return v

    def tick(self, ins):
        ins.then_inc(self.sem, 1)
        self.k = self.k + 1
        self.written += 1

    def link(self, ins):
        self.tick(ins)
        self.engine.wait_ge(self.sem, self.value())

    @contextmanager
    def loop(self, start, end, per, nested=False):
        k0, w0 = self.k, self.written
        with self.engine.Fori(start, end) as i:
            self.terms.append((i, start, per))
            yield i
            assert nested or self.written - w0 == per, (self.written - w0, per)
            self.terms.pop()
        self.k = k0 + (end - start) * per


def cols(t, c, width=1):
    return t[:, bass.ds(c * (C * width), C * width)]


def copy(nc, out, in_):
    return nc.vector.tensor_scalar(out, in_, 1.0, None, ALU.mult)


def rows3(ap, d=D):
    return ap.rearrange("p (j f) -> p j f", f=d)


def spread(ap, d=D):
    n = ap.shape[1]
    return ap.rearrange("p (n a) -> p n a", a=1).broadcast_to([ap.shape[0], n, d])


def spread1(ap, d=D):
    return ap.unsqueeze(2).broadcast_to([ap.shape[0], ap.shape[1], d])


def repeat(ap, n):
    return ap.rearrange("p (a d) -> p a d", a=1).broadcast_to([ap.shape[0], n, ap.shape[1]])


def build(nc, x, src_pe, dst_pe, dst_prev, dst_next, attr3, attr10t, weight, beta, W1, W2, vecs,
          fc1_w1, fc1_w2, fc2_w1, fc2_w2, out):
    T1 = nc.dram_tensor("T1", (N, D), F32, kind="Internal").ap()
    T2 = nc.dram_tensor("T2", (N, D), F32, kind="Internal").ap()
    T3 = nc.dram_tensor("T3", (N, D), F32, kind="Internal").ap()
    NT = nc.dram_tensor("NT", (P * 784, 2), F32, kind="Internal").ap()
    U = nc.dram_tensor("U", (EP + 1, UW), F32, kind="Internal").ap()
    LIVE = nc.dram_tensor("LIVE", (EP, 4), F32, kind="Internal").ap()
    UL = nc.dram_tensor("UL", (EP + 1, D), F32, kind="Internal").ap()
    LS = nc.dram_tensor("LS", (EP, D), F32, kind="Internal").ap()
    X2 = nc.dram_tensor("X2", (P, J * D), F32, kind="Internal").ap()
    sorted_src = nc.dram_tensor("sorted_src", (EP + 2,), F32, kind="Internal").ap()
    sorted_dst = nc.dram_tensor("sorted_dst", (EP,), F32, kind="Internal").ap()
    top = ExitStack()

    def sb(ctx, name, shape, dt=F32):
        return ctx.enter_context(nc.sbuf_tensor(name, shape, dt))

    def ps(ctx, name, shape, dt=F32):
        return ctx.enter_context(nc.psum_tensor(name, shape, dt))

    in_use = []
    begun = nc.alloc_semaphore(name="begun")

    def sem(ctx, name):
        in_use.append(nc.alloc_semaphore(name=name))
        return in_use[-1]

    def recycle():
        nc.clear_and_free_semaphores(in_use)
        in_use.clear()
        nc.all_engine_barrier()

    with top:
        R1 = sb(top, "R1", [P, J * D])
        R2 = sb(top, "R2", [P, J * D])
        lay = ExitStack()
        slots = [sb(top, f"slot{s}", [P, C * 2 * D]) for s in range(2)]
        islots = [sb(top, f"islot{s}", [P, 2 * C], I32) for s in range(2)]
        ident = sb(top, "ident", [P, P])
        ones = sb(top, "ones", [P, P])
        pos = sb(top, "pos", [P, J])
        contD, nendD, FD = (sb(top, n, [P, J]) for n in ("contD", "nendD", "FD"))
        sidxD, srcD, dstD = (sb(top, n, [P, J], I32) for n in ("sidxD", "srcD", "dstD"))
        ATD = sb(top, "ATD", [D, P])
        carry = sb(top, "carry", [P, D])
        crow = sb(top, "crow", [D, P + 1])
        vec = sb(top, "vec", [P, 7 * D])
        b1v, g1v, be1v, b2v, g2v, be2v = (vec[:, i * D:(i + 1) * D] for i in range(6))
        betav = vec[:, 6 * D:6 * D + 1]
        R3 = sb(lay, "R3", [P, (J + 1) * D])
        SCRATCH = 5120


        def dense_act(act, eps, src_t, dst_t, s, din, dout, tmp):
            dst_v = dst_t[0:DENSE * NODES_CH, :].rearrange("(k p r) f -> k p (r f)", p=P, r=R)
            src_v = src_t[0:DENSE * NODES_CH, :].rearrange("(k p r) f -> k p (r f)", p=P, r=R)
            dst_l = dst_t[DENSE * NODES_CH:N, :].rearrange("(p r) f -> p (r f)", r=R)
            src_l = src_t[DENSE * NODES_CH:N, :].rearrange("(p r) f -> p (r f)", r=R)
            ld, var_ready, std_ready, y_ready, st = s
            var, std = tmp

            def chunk(k, q, load, store, np_=P):
                act.wait_ge(var_ready, k + 1)
                nc.scalar.activation(std[0:np_, :], var[0:np_, :], ACT.Sqrt, bias=eps[0:np_, :],
                                     scale=1.0 / D).then_inc(std_ready, 1)
                if load is not None:
                    act.dma_start(din[q][0:load[1], :], load[0]).then_inc(ld[q], 16)
                act.wait_ge(y_ready, k + 1)
                act.dma_start(store, dout[q][0:np_, :]).then_inc(st[q], 16)

            act.dma_start(din[0][:, :], src_v[0]).then_inc(ld[0], 16)
            act.dma_start(din[1][:, :], src_v[1]).then_inc(ld[1], 16)
            with act.Fori(0, DENSE // 2 - 1) as i:
                for q in range(2):
                    k = i * 2 + q
                    chunk(k, q, (src_v[bass.ds(k + 2, 1)].rearrange("a p n -> (a p) n"), P),
                          dst_v[bass.ds(k, 1)].rearrange("a p n -> (a p) n"))
            chunk(DENSE - 2, 0, (src_l, TAILP), dst_v[DENSE - 2])
            chunk(DENSE - 1, 1, None, dst_v[DENSE - 1])
            chunk(DENSE, 0, None, dst_l, TAILP)
            act.wait_ge(st[0], 16 * (DENSE // 2 + 1))
            act.wait_ge(st[1], 16 * (DENSE // 2))

        def dense_dve(dve, ch, s, din, dout, tmp, small):
            ld, var_ready, std_ready, y_ready, st = s
            var, std = tmp
            total, rstd, centred, sq = small

            def chunk(i, q, first=False, np_=P):
                dve.wait_ge(ld[q], i * 16 + 16)
                xin = rows3(din[q][0:np_, :])
                ch.link(nc.vector.tensor_reduce(total[0:np_, :], xin, AX, ALU.add))
                ch.link(nc.vector.scalar_tensor_tensor(rows3(centred[0:np_, :]), spread(total[0:np_, :]),
                                                       -1.0 / D, xin, ALU.mult, ALU.add))
                ch.link(nc.vector.tensor_tensor(sq[0:np_, :], centred[0:np_, :], centred[0:np_, :], ALU.mult))
                nc.vector.tensor_reduce(var[0:np_, :], rows3(sq[0:np_, :]), AX, ALU.add).then_inc(var_ready, 1)
                dve.wait_ge(std_ready, i * 2 + q + 1)
                ch.link(nc.vector.reciprocal(rstd[0:np_, :], std[0:np_, :]))
                if not first:
                    dve.wait_ge(st[q], i * 16)
                nc.vector.tensor_tensor(rows3(dout[q][0:np_, :]), rows3(centred[0:np_, :]),
                                        spread(rstd[0:np_, :]), ALU.mult).then_inc(y_ready, 1)
                dve.wait_ge(y_ready, i * 2 + q + 1)

            chunk(0, 0, first=True)
            chunk(0, 1, first=True)
            with ch.loop(1, DENSE // 2, 8) as i:
                chunk(i, 0)
                chunk(i, 1)
            chunk(DENSE // 2, 0, np_=TAILP)

        @contextmanager
        def dense_buffers(ctx, tag):
            at = [SCRATCH]

            def part(n):
                at[0] += n
                return R3[:, at[0] - n:at[0]]

            din, dout = [part(R * D), part(R * D)], [part(R * D), part(R * D)]
            tmp = (part(R), part(R))
            small = (part(R), part(R), part(R * D), part(R * D))
            s = ([sem(ctx, f"dense_ld{q}_{tag}") for q in range(2)], sem(ctx, f"dense_var_{tag}"),
                 sem(ctx, f"dense_std_{tag}"), sem(ctx, f"dense_y_{tag}"),
                 [sem(ctx, f"dense_st{q}_{tag}") for q in range(2)])
            yield din, dout, tmp, small, s

        def stage_indices(sp, taken, staged, index_tiles):
            with sp.Fori(0, HALF) as i:
                for q in range(2):
                    sp.wait_ge(taken, i * 2 + q + 1)
                    for n, t in enumerate(index_tiles):
                        sp.dma_start(islots[q][:, n * C:(n + 1) * C], cols(t, i * 2 + q)).then_inc(staged[q], 16)

        def gather(pool, i, q, got, tables, width, per, stride=None):
            stride = stride or width * len(tables)
            for j in range(C):
                for n, t in enumerate(tables):
                    o = j * stride + n * width
                    pool.indirect_dma_start(slots[q][:, o:o + width], None, t,
                                            bass.IndirectOffsetOnAxis(ap=islots[q][:, n * C + j:n * C + j + 1], axis=0),
                                            bounds_check=per, oob_is_err=False).then_inc(got[q], 16)

        def gather_pass(pool, staged, got, tables, width, limit):
            limit = pool.to_reg(limit)
            with pool.Fori(0, HALF) as i:
                for q in range(2):
                    pool.wait_ge(staged[q], i * (16 * len(tables)) + 16 * len(tables))
                    pool.sem_inc(begun, 1)
                    gather(pool, i, q, got, tables, width, limit)

        def scatter_pass(pool, filled, sent, table, width):
            limit = pool.to_reg(MAXROW)
            with pool.Fori(0, HALF) as i:
                for q in range(2):
                    pool.wait_ge(filled, i * 2 + q + 1)
                    pool.sem_inc(begun, 1)
                    for j in range(C):
                        pool.indirect_dma_start(table, bass.IndirectOffsetOnAxis(ap=islots[q][:, j:j + 1], axis=0),
                                                slots[q][:, j * width:(j + 1) * width], None,
                                                bounds_check=limit, oob_is_err=False).then_inc(sent[q], 16)
            for q in range(2):
                pool.wait_ge(sent[q], 16 * C * HALF)

        def feature_scan(ch, cont, m, Rs):
            for f in range(D):
                ins = nc.vector.tensor_tensor_scan(Rs[:, D + f:D + f + (J - 1) * D + 1:D], cont[:, :],
                                                   m[:, f:f + (J - 1) * D + 1:D], 0.0, ALU.mult, ALU.add)
                ch.tick(ins)
            dve = ch.engine
            dve.wait_ge(ch.sem, ch.value())

        def chain_sems(ctx, tag):
            return [sem(ctx, f"{n}_{tag}") for n in ("last_ready", "row_ready", "chained", "back")]

        def carries_dve(ch, s, n, w, AT, pst, psb, dst, op0, op1, start, backward=False):
            dve = ch.engine
            _, row_ready, chained, back = s
            dve.wait_ge(row_ready, n + 1)
            if backward:
                ch.link(nc.vector.memset(crow[0:w, P:P + 1], start))
                nc.vector.tensor_tensor_scan(crow[0:w, P - 1::-1], AT[0:w, P - 1::-1], pst[0:w, P - 1::-1],
                                             start, op0, op1).then_inc(chained, 1)
            else:
                ch.link(nc.vector.memset(crow[0:w, 0:1], start))
                nc.vector.tensor_tensor_scan(crow[0:w, 1:P + 1], AT[0:w, :], pst[0:w, :],
                                             start, op0, op1).then_inc(chained, 1)
            dve.wait_ge(back, n + 1)
            ch.link(nc.vector.tensor_copy(dst, psb[:, 0:w]))

        def carries_pe(pe, s, n, w, last, pst, psb, backward=False):
            last_ready, row_ready, chained, back = s
            pe.wait_ge(last_ready, n + 1)
            nc.tensor.transpose(pst[0:w, :], last, ident[:, :]).then_inc(row_ready, 1)
            pe.wait_ge(chained, n + 1)
            o = 1 if backward else 0
            if isinstance(n, int):
                nc.tensor.transpose(psb[:, 0:w], crow[0:w, o:o + P], ident[0:w, 0:w]).then_inc(back, 1)
            else:
                nc.tensor.matmul(psb[:, 0:w], crow[0:w, o:o + P], ident[0:w, 0:w], start=True,
                                 stop=True).then_inc(back, 1)

        def flags_dve(ch, key, prev, nxt, cont, nend, F, sidx, tmp):
            ch.link(nc.vector.tensor_tensor(cont[:, :], key, prev, ALU.is_equal))
            ch.link(nc.vector.tensor_tensor(nend[:, :], key, nxt, ALU.is_equal))
            ch.link(nc.vector.tensor_tensor_scan(F[:, :], cont[:, :], cont[:, :], 1.0, ALU.mult, ALU.min))
            ch.link(nc.vector.tensor_scalar(tmp[:, :], key, -1.0, float(N), ALU.mult, ALU.add))
            ch.link(nc.vector.tensor_tensor(tmp[:, :], tmp[:, :], nend[:, :], ALU.mult))
            ch.link(nc.vector.tensor_tensor(tmp[:, :], tmp[:, :], key, ALU.add))
            ch.link(nc.vector.tensor_copy(sidx[:, :], tmp[:, :]))

        def finish(tag, own, Rs, F, sidx, table, own_scale=1.0, sum_scale=None, rowscale=None, keep=False,
                   plus=None):
            with ExitStack() as ctx:
                filled = sem(ctx, f"filled_{tag}")
                var_ready, std_ready = sem(ctx, f"var_{tag}"), sem(ctx, f"std_{tag}")
                sent = [sem(ctx, f"sent{q}_{tag}") for q in range(2)]
                step = sem(ctx, f"dve_{tag}")
                t = sb(ctx, f"t_{tag}", [P, CD])
                sq = sb(ctx, f"sq_{tag}", [P, CD])
                tot, var, std, rstd, eps = (sb(ctx, f"{n}_{tag}", [P, C]) for n in ("tot", "var", "std", "rstd", "eps"))
                block = ctx.enter_context(nc.Block())

                @block.gpsimd
                def _(pool):
                    scatter_pass(pool, filled, sent, table, D)

                @block.scalar
                def _(act):
                    act.wait_ge(step, 1)
                    with act.Fori(0, NCH) as c:
                        act.wait_ge(var_ready, c + 1)
                        nc.scalar.activation(std[:, :], var[:, :], ACT.Sqrt, bias=eps[:, 0:1],
                                             scale=1.0 / D).then_inc(std_ready, 1)

                @block.vector
                def _(dve):
                    ch = Chain(dve, step)
                    ch.link(nc.vector.memset(eps[:, :], LNEPS))

                    def chunk(i, q, first=False):
                        c = i * 2 + q
                        if plus is None:
                            ch.link(nc.vector.tensor_tensor(rows3(t[:, :]), spread(cols(F, c)), repeat(carry[:, :], C), ALU.mult))
                            ch.link(nc.vector.tensor_tensor(t[:, :], t[:, :], Rs[:, bass.ds(c * CD + D, CD)], ALU.add))
                        else:
                            ch.link(nc.vector.scalar_tensor_tensor(t[:, :], Rs[:, bass.ds(c * CD + D, CD)], ALPHA,
                                                                   cols(plus, c, D), ALU.mult, ALU.add))
                        if rowscale is not None:
                            ch.link(nc.vector.tensor_tensor(rows3(t[:, :]), rows3(t[:, :]), spread(cols(rowscale, c)), ALU.mult))
                        if sum_scale is not None:
                            ch.link(nc.vector.tensor_scalar(t[:, :], t[:, :], sum_scale, None, ALU.mult))
                        ch.link(nc.vector.scalar_tensor_tensor(t[:, :], cols(own, c, D), own_scale, t[:, :], ALU.mult, ALU.add))
                        ch.link(nc.vector.tensor_reduce(tot[:, :], rows3(t[:, :]), AX, ALU.add))
                        ch.link(nc.vector.scalar_tensor_tensor(rows3(t[:, :]), spread(tot[:, :]), -1.0 / D, rows3(t[:, :]), ALU.mult, ALU.add))
                        ch.link(nc.vector.tensor_tensor(sq[:, :], t[:, :], t[:, :], ALU.mult))
                        nc.vector.tensor_reduce(var[:, :], rows3(sq[:, :]), AX, ALU.add).then_inc(var_ready, 1)
                        dve.wait_ge(std_ready, c + 1)
                        ch.link(nc.vector.reciprocal(rstd[:, :], std[:, :]))
                        if not first:
                            dve.wait_ge(sent[q], i * (16 * C))
                        if keep:
                            ch.link(nc.vector.tensor_tensor(rows3(cols(own, c, D)), rows3(t[:, :]), spread(rstd[:, :]), ALU.mult))
                            ch.link(copy(nc, slots[q][:, 0:CD], cols(own, c, D)))
                        else:
                            ch.link(nc.vector.tensor_tensor(rows3(slots[q][:, 0:CD]), rows3(t[:, :]), spread(rstd[:, :]), ALU.mult))
                        nc.vector.tensor_copy(islots[q][:, 0:C], cols(sidx, c)).then_inc(filled, 1)
                        dve.wait_ge(filled, c + 1)

                    per = 2 * (8 - (plus is not None) + (rowscale is not None) + (sum_scale is not None) + keep)
                    chunk(0, 0, True)
                    chunk(0, 1, True)
                    with ch.loop(1, HALF, per) as i:
                        chunk(i, 0)
                        chunk(i, 1)

        with ExitStack() as ctx:
            keyf, prevf, nextf, tmp = (sb(ctx, n, [P, J]) for n in ("keyf", "prevf", "nextf", "tmp0"))
            prevD, nextD, posi = (sb(ctx, n, [P, J], I32) for n in ("prevD", "nextD", "posi"))
            fill = sb(ctx, "fill", [P, 784 * 2])
            minus = sb(ctx, "minus", [1, D])
            zero = sb(ctx, "zero", [1, UW])
            none = sb(ctx, "none", [P, J * 4])
            arep = sb(ctx, "arep", [P, D])
            pst = ps(ctx, "pst0", [P, P])
            loaded, stored, made, step0, arep_ready, at_ready = (sem(ctx, n) for n in (
                "loaded0", "stored0", "made0", "dve_0", "arep0", "at0"))
            with nc.Block() as block:
                @block.sync
                def _(sp):
                    for d_, s_ in ((srcD, src_pe), (dstD, dst_pe), (prevD, dst_prev), (nextD, dst_next), (vec, vecs)):
                        sp.dma_start(d_[:, :], s_).then_inc(loaded, 16)
                    sp.wait_ge(step0, 9)
                    sp.dma_start(NT.rearrange("(p n) t -> p (n t)", p=P), fill[:, :]).then_inc(stored, 16)
                    sp.dma_start(U[EP:EP + 1, :], zero[:, :]).then_inc(stored, 16)
                    sp.dma_start(UL[EP:EP + 1, :], zero[:, 0:D]).then_inc(stored, 16)
                    sp.dma_start(LIVE.rearrange("(p n) t -> p (n t)", p=P), none[:, :]).then_inc(stored, 16)
                    ends = sorted_src.rearrange("(a n) -> a n", a=1)
                    sp.dma_start(ends[:, 0:1], minus[:, 0:1]).then_inc(stored, 16)
                    sp.dma_start(ends[:, EP + 1:EP + 2], minus[:, 0:1]).then_inc(stored, 16)
                    sp.wait_ge(stored, 96)

                @block.gpsimd
                def _(pool):
                    nc.gpsimd.memset(ident[:, :], 0.0).then_inc(made, 1)
                    nc.gpsimd.memset(ones[:, :], 1.0).then_inc(made, 1)
                    pool.wait_ge(made, 2)
                    nc.gpsimd.affine_select(out=ident[:, :], in_=ident[:, :], compare_op=ALU.not_equal, fill=1.0,
                                            base=0, pattern=[[-1, P]], channel_multiplier=1).then_inc(made, 1)
                    nc.gpsimd.iota(posi[:, :], pattern=[[1, J]], base=0, channel_multiplier=J).then_inc(made, 1)
                    nc.gpsimd.memset(slots[0][:, :], 1.0).then_inc(made, 1)
                    nc.gpsimd.memset(slots[1][:, :], 1.0).then_inc(made, 1)

                @block.vector
                def _(dve):
                    ch = Chain(dve, step0)
                    ch.link(nc.vector.memset(fill[:, 1:784 * 2:2], 1.0))
                    ch.link(nc.vector.memset(fill[:, 0:784 * 2:2], float(EP)))
                    ch.link(nc.vector.memset(minus[:, :], -1.0))
                    ch.link(nc.vector.memset(zero[:, :], 0.0))
                    ch.link(nc.vector.memset(zero[:, D:UW], float(EP)))
                    for n, value in enumerate((float(EP), 0.0, 1.0, float(N))):
                        ch.link(nc.vector.memset(none[:, n:J * 4:4], value))
                    dve.wait_ge(loaded, 80)
                    ch.link(nc.vector.tensor_copy(keyf[:, :], dstD[:, :]))
                    ch.link(nc.vector.tensor_copy(prevf[:, :], prevD[:, :]))
                    ch.link(nc.vector.tensor_copy(nextf[:, :], nextD[:, :]))
                    dve.wait_ge(made, 6)
                    ch.link(nc.vector.tensor_copy(pos[:, :], posi[:, :]))
                    flags_dve(ch, keyf[:, :], prevf[:, :], nextf[:, :], contD, nendD, FD, sidxD, tmp)
                    nc.vector.tensor_copy(arep[:, :], FD[:, J - 1:J].broadcast_to([P, D])).then_inc(arep_ready, 1)
                    dve.wait_ge(at_ready, 1)
                    ch.link(nc.vector.tensor_copy(ATD[:, :], pst[0:D, :]))

                @block.tensor
                def _(pe):
                    pe.wait_ge(made, 6)
                    pe.wait_ge(arep_ready, 1)
                    nc.tensor.transpose(pst[0:D, :], arep[:, :], ident[:, :]).then_inc(at_ready, 1)

        scal = ExitStack()
        nrm_s, nrm_d, dot = (sb(scal, n, [P, J]) for n in ("nrm_s", "nrm_d", "dot"))
        with ExitStack() as ctx:
            K, V = ([R3[:, (2 * n + b) * SORTW:(2 * n + b + 1) * SORTW] for b in range(2)] for n in range(2))
            above, diff = (R3[:, 4 * SORTW + n * (SORTW // 2):4 * SORTW + (n + 1) * (SORTW // 2)] for n in range(2))
            sign = R3[:, 5 * SORTW:6 * SORTW]
            place, bits = (R3[:, n * SORTW:(n + 1) * SORTW].bitcast(I32) for n in (6, 7))
            prod = sb(ctx, "prod1", [P, CD])
            eps1 = sb(ctx, "eps1", [P, 1])
            kT, vT = ps(ctx, "kT", [P, SORTW]), ps(ctx, "vT", [P, SORTW])
            taken, kept, placed, turn, turned, sorted_, stored, step1 = (sem(ctx, n) for n in (
                "taken1", "kept1", "placed1", "turn1", "turned1", "sorted1", "stored1", "dve_1"))
            staged = [sem(ctx, f"staged{q}_1") for q in range(2)]
            copied = [sem(ctx, f"copied{q}_1") for q in range(2)]
            got = [sem(ctx, f"got{q}_1") for q in range(2)]
            with dense_buffers(ctx, "t1") as (din, dout, tmp, small, ds_), nc.Block() as block:
                @block.gpsimd
                def _(pool):
                    nc.gpsimd.iota(place[:, :], pattern=[[1, SORTW]], base=0, channel_multiplier=SORTW).then_inc(placed, 1)
                    gather_pass(pool, staged, got, (x, x), D, MAXROW)

                @block.sync
                def _(sp):
                    def indices(c, q):
                        sp.dma_start(islots[q][:, 0:C], cols(srcD, c)).then_inc(staged[q], 16)
                        sp.dma_start(islots[q][:, C:2 * C], cols(dstD, c)).then_inc(staged[q], 16)

                    def keep(i, q):
                        c = i * 2 + q
                        sp.wait_ge(got[q], i * (32 * C) + 32 * C)
                        both = slots[q][:, :].rearrange("p (j t f) -> p j t f", t=2, f=D)
                        sp.dma_start(rows3(cols(R1, c, D)), both[:, :, 0, :]).then_inc(copied[q], 16)
                        sp.dma_start(rows3(cols(R2, c, D)), both[:, :, 1, :]).then_inc(copied[q], 16)
                        sp.wait_ge(copied[q], i * 32 + 32)

                    indices(0, 0)
                    indices(1, 1)
                    with sp.Fori(0, HALF - 1) as i:
                        for q in range(2):
                            keep(i, q)
                            indices(i * 2 + q + 2, q)
                    keep(HALF - 1, 0)
                    keep(HALF - 1, 1)
                    sp.wait_ge(sorted_, 1)
                    sp.dma_start(sorted_src[1:EP + 1].rearrange("(p n) -> p n", p=SORTP), K[0][0:SORTP, :]).then_inc(stored, 16)
                    sp.dma_start(sorted_dst.rearrange("(p n) -> p n", p=SORTP), V[0][0:SORTP, :]).then_inc(stored, 16)
                    sp.wait_ge(stored, 32)

                @block.scalar
                def _(act):
                    act.wait_ge(step1, 1)
                    dense_act(act, eps1, x, T1, ds_, din, dout, tmp)

                @block.tensor
                def _(pe):
                    for n in range(2 * (LOG - 9)):
                        pe.wait_ge(turn, n + 1)
                        for q in range(4):
                            b = slice(q * P, (q + 1) * P)
                            nc.tensor.transpose(kT[:, b], K[0][:, b], ident[:, :])
                            last = nc.tensor.transpose(vT[:, b], V[0][:, b], ident[:, :])
                        last.then_inc(turned, 1)

                @block.vector
                def _(dve):
                    ch = Chain(dve, step1)
                    ch.link(nc.vector.memset(eps1[:, :], LNEPS))
                    dense_dve(dve, ch, ds_, din, dout, tmp, small)
                    for b, t in ((K, srcD), (V, dstD)):
                        ch.link(nc.vector.memset(b[0][:, J:SORTW], float(N)))
                        ch.link(nc.vector.tensor_copy(b[0][:, 0:J], t[:, :]))
                    dve.wait_ge(placed, 1)
                    ch.link(nc.vector.tensor_single_scalar(bits[:, :], place[:, :], 1, ALU.logical_shift_right))
                    ch.link(nc.vector.tensor_tensor(place[:, :], place[:, :], bits[:, :], ALU.bitwise_xor))
                    ch.link(nc.vector.tensor_single_scalar(bits[:, :], bits[:, :], 1, ALU.bitwise_and))
                    turns = [0]
                    now = [0]

                    def transpose():
                        if now[0] == 1:
                            ch.link(nc.vector.tensor_copy(K[0][:, :], K[1][:, :]))
                            ch.link(nc.vector.tensor_copy(V[0][:, :], V[1][:, :]))
                            now[0] = 0
                        dve.sem_inc(turn, 1)
                        turns[0] += 1
                        dve.wait_ge(turned, turns[0])
                        ch.tick(nc.vector.tensor_copy(K[0][:, :], kT[:, :]))
                        ch.link(nc.vector.tensor_copy(V[0][:, :], vT[:, :]))

                    def compare(stride):
                        a, b = now[0], 1 - now[0]
                        kk, vv, kn, vn = (t[:, :].rearrange("p (n t s) -> p n t s", t=2, s=stride)
                                          for t in (K[a], V[a], K[b], V[b]))
                        ab, df = (t[:, :].rearrange("p (n s) -> p n s", s=stride) for t in (above, diff))
                        ch.tick(nc.vector.tensor_tensor(df, vv[:, :, 1], vv[:, :, 0], ALU.subtract))
                        ch.tick(nc.vector.tensor_tensor(ab, kk[:, :, 0], kk[:, :, 1], ALU.is_gt))
                        ch.tick(nc.vector.tensor_tensor(kn[:, :, 0], kk[:, :, 0], kk[:, :, 1], ALU.min))
                        ch.link(nc.vector.tensor_tensor(kn[:, :, 1], kk[:, :, 0], kk[:, :, 1], ALU.max))
                        ch.link(nc.vector.tensor_tensor(df, df, ab, ALU.mult))
                        ch.tick(nc.vector.tensor_tensor(vn[:, :, 0], vv[:, :, 0], df, ALU.add))
                        ch.link(nc.vector.tensor_tensor(vn[:, :, 1], vv[:, :, 1], df, ALU.subtract))
                        now[0] = b

                    for k in range(1, LOG + 1):
                        if k > 1:
                            ch.link(nc.vector.tensor_scalar(bits[:, :], place[:, :], k - 1, 1,
                                                            ALU.logical_shift_right, ALU.bitwise_and))
                        ch.link(nc.vector.tensor_scalar(sign[:, :], bits[:, :], -2.0, 1.0, ALU.mult, ALU.add))
                        ch.link(nc.vector.tensor_tensor(K[now[0]][:, :], K[now[0]][:, :], sign[:, :], ALU.mult))
                        if k > 9:
                            transpose()
                            for b in range(k - 1, 8, -1):
                                compare(1 << (b - 9))
                            transpose()
                        for b in range(min(k, 9) - 1, -1, -1):
                            compare(1 << b)
                    if now[0] == 1:
                        ch.link(nc.vector.tensor_copy(K[0][:, :], K[1][:, :]))
                        ch.link(nc.vector.tensor_copy(V[0][:, :], V[1][:, :]))
                    dve.sem_inc(sorted_, 1)

                    with ch.loop(0, HALF, 12) as i:
                        for q in range(2):
                            c = i * 2 + q
                            dve.wait_ge(copied[q], i * 32 + 32)
                            for a, b, o in ((R1, R1, nrm_s), (R2, R2, nrm_d), (R1, R2, dot)):
                                ch.link(nc.vector.tensor_tensor(prod[:, :], cols(a, c, D), cols(b, c, D), ALU.mult))
                                ch.link(nc.vector.tensor_reduce(cols(o, c), rows3(prod[:, :]), AX, ALU.add))

        with ExitStack() as ctx:
            e_, m_, mask_, t_ = (sb(ctx, n, [P, J]) for n in ("e2", "m2", "mask2", "t2"))
            ccol = sb(ctx, "ccol", [P, 1])
            brow = sb(ctx, "brow", [P, 1])
            AB, AM = sb(ctx, "AB", [1, P]), sb(ctx, "AM", [1, P])
            pst, psb = ps(ctx, "pst2", [P, P]), ps(ctx, "psb2", [P, D])
            cs = chain_sems(ctx, "2")
            last_ready = cs[0]
            step2, rooted, expd, asked = (sem(ctx, n) for n in ("dve_2", "rooted2", "exp2", "asked2"))
            with nc.Block() as block:
                @block.scalar
                def _(act):
                    act.wait_ge(asked, 1)
                    nc.scalar.activation(nrm_s[:, :], nrm_s[:, :], ACT.Sqrt).then_inc(rooted, 1)
                    nc.scalar.activation(nrm_d[:, :], nrm_d[:, :], ACT.Sqrt).then_inc(rooted, 1)
                    act.wait_ge(asked, 2)
                    nc.scalar.activation(dot[:, :], e_[:, :], ACT.Exp).then_inc(expd, 1)

                @block.tensor
                def _(pe):
                    pe.wait_ge(last_ready, 1)
                    nc.tensor.transpose(pst[0:1, :], brow[:, :], ident[:, :]).then_inc(cs[1], 1)
                    pe.wait_ge(cs[2], 1)
                    nc.tensor.transpose(psb[:, 0:1], crow[0:1, 0:P], ident[0:1, 0:1]).then_inc(cs[3], 1)
                    carries_pe(pe, cs, 1, 1, m_[:, J - 1:J], pst, psb)
                    carries_pe(pe, cs, 2, 1, t_[:, 0:1], pst, psb, backward=True)
                    carries_pe(pe, cs, 3, 1, t_[:, J - 1:J], pst, psb)
                    carries_pe(pe, cs, 4, D, R3[:, J * D:(J + 1) * D], pst, psb)

                @block.vector
                def _(dve):
                    ch = Chain(dve, step2)
                    v = nc.vector
                    ch.tick(v.tensor_scalar(nrm_s[:, :], nrm_s[:, :], 1e-24, None, ALU.max))
                    ch.link(v.tensor_scalar(nrm_d[:, :], nrm_d[:, :], 1e-24, None, ALU.max))
                    dve.sem_inc(asked, 1)
                    ch.link(v.tensor_tensor_scan(t_[:, J - 1::-1], nendD[:, J - 1::-1], nendD[:, J - 1::-1], 1.0, ALU.mult, ALU.min))
                    ch.link(v.tensor_copy(brow[:, :], t_[:, 0:1]))
                    ch.link(v.memset(crow[:, :], 0.0))
                    dve.sem_inc(last_ready, 1)
                    dve.wait_ge(cs[1], 1)
                    ch.link(v.tensor_copy(AB[:, :], pst[0:1, :]))
                    ch.link(v.tensor_scalar(AM[:, :], ATD[0:1, :], -1.0, BIG, ALU.add, ALU.mult))
                    dve.sem_inc(cs[2], 1)
                    dve.wait_ge(cs[3], 1)
                    ch.link(v.memset(R3[:, 0:D], 0.0))
                    ch.link(v.tensor_scalar(mask_[:, :], contD[:, :], -1.0, BIG, ALU.add, ALU.mult))
                    dve.wait_ge(rooted, 2)
                    ch.link(v.tensor_tensor(nrm_s[:, :], nrm_s[:, :], nrm_d[:, :], ALU.mult))
                    ch.link(v.reciprocal(nrm_s[:, :], nrm_s[:, :]))
                    ch.link(v.tensor_tensor(e_[:, :], dot[:, :], nrm_s[:, :], ALU.mult))
                    ch.link(v.tensor_scalar(e_[:, :], e_[:, :], betav, None, ALU.mult))
                    ch.link(v.tensor_tensor_scan(m_[:, :], mask_[:, :], e_[:, :], -BIG, ALU.add, ALU.max))
                    dve.sem_inc(last_ready, 1)
                    carries_dve(ch, cs, 1, 1, AM, pst, psb, ccol[:, :], ALU.add, ALU.max, -BIG)
                    ch.link(v.tensor_tensor_scan(m_[:, :], mask_[:, :], e_[:, :], ccol[:, :], ALU.add, ALU.max))
                    ch.link(v.tensor_scalar(mask_[:, :], nendD[:, :], -1.0, 1.0, ALU.mult, ALU.add))
                    ch.link(v.tensor_tensor(mask_[:, :], mask_[:, :], m_[:, :], ALU.mult))
                    ch.link(v.tensor_tensor_scan(t_[:, J - 1::-1], nendD[:, J - 1::-1], mask_[:, J - 1::-1], 0.0, ALU.mult, ALU.add))
                    dve.sem_inc(last_ready, 1)
                    carries_dve(ch, cs, 2, 1, AB, pst, psb, ccol[:, :], ALU.mult, ALU.add, 0.0, backward=True)
                    ch.link(v.tensor_tensor_scan(t_[:, J - 1::-1], nendD[:, J - 1::-1], mask_[:, J - 1::-1], ccol[:, :], ALU.mult, ALU.add))
                    ch.link(v.tensor_tensor(e_[:, :], e_[:, :], t_[:, :], ALU.subtract))
                    dve.sem_inc(asked, 1)
                    dve.wait_ge(expd, 1)
                    ch.link(v.tensor_tensor_scan(t_[:, :], contD[:, :], dot[:, :], 0.0, ALU.mult, ALU.add))
                    dve.sem_inc(last_ready, 1)
                    carries_dve(ch, cs, 3, 1, ATD, pst, psb, ccol[:, :], ALU.mult, ALU.add, 0.0)
                    ch.link(v.tensor_tensor_scan(t_[:, :], contD[:, :], dot[:, :], ccol[:, :], ALU.mult, ALU.add))
                    ch.link(v.reciprocal(nrm_d[:, :], t_[:, :]))
                    ch.link(v.tensor_tensor(rows3(R1[:, :]), rows3(R1[:, :]), spread(dot[:, :]), ALU.mult))
                    feature_scan(ch, contD, R1, R3)
                    dve.sem_inc(last_ready, 1)
                    carries_dve(ch, cs, 4, D, ATD, pst, psb, carry[:, :], ALU.mult, ALU.add, 0.0)

        finish("l0", R2, R3, FD, sidxD, T1, rowscale=nrm_d)
        scal.close()

        recycle()
        ordS = ExitStack()
        contS, FS, degrow = (sb(ordS, n, [P, J]) for n in ("contS", "FS", "degrow"))
        valid = sb(ordS, "valid", [P, J])
        sidxS, srcS, dstS = (sb(ordS, n, [P, J], I32) for n in ("sidxS", "srcS", "dstS"))
        ATS = sb(ordS, "ATS", [D, P])
        nendS, endpos = sb(ordS, "nendS", [P, J]), sb(ordS, "endpos", [P, J])
        ABS = sb(ordS, "ABS", [1, P])
        PD = sb(ordS, "PD", [P, J * 2])
        with ExitStack() as ctx:
            keyf, prevf, nextf, tmp, cnt, t_ = (R3[:, D + n * J:D + (n + 1) * J] for n in range(6))
            ccol, brow = sb(ctx, "ccol4", [P, 1]), sb(ctx, "brow4", [P, 1])
            arep = sb(ctx, "arep4", [P, D])
            eps1 = sb(ctx, "eps4", [P, 1])
            pst, psb = ps(ctx, "pst4", [P, P]), ps(ctx, "psb4", [P, D])
            cs = chain_sems(ctx, "4")
            last_ready = cs[0]
            step4, loaded, filled = (sem(ctx, n) for n in ("dve_4", "loaded4", "filled4"))
            sent = [sem(ctx, f"sent{q}_4") for q in range(2)]
            with dense_buffers(ctx, "t2") as (din, dout, dtmp, small, ds_), nc.Block() as block:
                @block.sync
                def _(sp):
                    for d_, s_ in ((prevf, sorted_src[0:EP]), (keyf, sorted_src[1:EP + 1]),
                                   (nextf, sorted_src[2:EP + 2]), (tmp, sorted_dst)):
                        sp.dma_start(d_, s_.rearrange("(p n) -> p n", p=P)).then_inc(loaded, 16)

                @block.gpsimd
                def _(pool):
                    scatter_pass(pool, filled, sent, NT, 2)

                @block.scalar
                def _(act):
                    act.wait_ge(step4, 1)
                    dense_act(act, eps1, T1, T2, ds_, din, dout, dtmp)

                @block.tensor
                def _(pe):
                    pe.wait_ge(last_ready, 1)
                    nc.tensor.transpose(pst[0:D, :], arep[:, :], ident[:, :]).then_inc(cs[1], 1)
                    pe.wait_ge(cs[2], 1)
                    nc.tensor.transpose(psb[:, 0:1], crow[0:1, 0:P], ident[0:1, 0:1]).then_inc(cs[3], 1)
                    pe.wait_ge(last_ready, 2)
                    nc.tensor.transpose(pst[0:1, :], brow[:, :], ident[:, :]).then_inc(cs[1], 1)
                    pe.wait_ge(cs[2], 2)
                    nc.tensor.transpose(psb[:, 0:1], crow[0:1, 0:P], ident[0:1, 0:1]).then_inc(cs[3], 1)
                    carries_pe(pe, cs, 2, 1, cnt[:, J - 1:J], pst, psb)
                    carries_pe(pe, cs, 3, 1, t_[:, 0:1], pst, psb, backward=True)

                @block.vector
                def _(dve):
                    v = nc.vector
                    ch = Chain(dve, step4)
                    ch.link(v.memset(eps1[:, :], LNEPS))
                    dve.wait_ge(loaded, 64)
                    ch.link(v.tensor_copy(srcS[:, :], keyf))
                    ch.link(v.tensor_copy(dstS[:, :], tmp))
                    ch.link(v.tensor_scalar(valid[:, :], keyf, float(N), None, ALU.is_lt))
                    flags_dve(ch, keyf, prevf, nextf, contS, nendS, FS, sidxS, tmp)
                    ch.link(v.tensor_copy(arep[:, :], FS[:, J - 1:J].broadcast_to([P, D])))
                    dve.sem_inc(last_ready, 1)
                    dve.wait_ge(cs[1], 1)
                    ch.link(v.tensor_copy(ATS[:, :], pst[0:D, :]))
                    dve.sem_inc(cs[2], 1)
                    dve.wait_ge(cs[3], 1)
                    ch.link(v.tensor_tensor_scan(t_[:, J - 1::-1], nendS[:, J - 1::-1], nendS[:, J - 1::-1], 1.0, ALU.mult, ALU.min))
                    ch.link(v.tensor_copy(brow[:, :], t_[:, 0:1]))
                    dve.sem_inc(last_ready, 1)
                    dve.wait_ge(cs[1], 2)
                    ch.link(v.tensor_copy(ABS[:, :], pst[0:1, :]))
                    dve.sem_inc(cs[2], 1)
                    dve.wait_ge(cs[3], 2)
                    ch.link(v.tensor_tensor_scan(cnt, contS[:, :], valid[:, :], 0.0, ALU.mult, ALU.add))
                    dve.sem_inc(last_ready, 1)
                    carries_dve(ch, cs, 2, 1, ATS, pst, psb, ccol[:, :], ALU.mult, ALU.add, 0.0)
                    ch.link(v.tensor_tensor_scan(cnt, contS[:, :], valid[:, :], ccol[:, :], ALU.mult, ALU.add))
                    ch.link(v.tensor_scalar(tmp, nendS[:, :], -1.0, 1.0, ALU.mult, ALU.add))
                    ch.link(v.tensor_tensor(tmp, tmp, cnt, ALU.mult))
                    ch.link(v.tensor_tensor_scan(t_[:, J - 1::-1], nendS[:, J - 1::-1], tmp[:, J - 1::-1], 0.0, ALU.mult, ALU.add))
                    dve.sem_inc(last_ready, 1)
                    carries_dve(ch, cs, 3, 1, ABS, pst, psb, ccol[:, :], ALU.mult, ALU.add, 0.0, backward=True)
                    ch.link(v.tensor_tensor_scan(degrow[:, J - 1::-1], nendS[:, J - 1::-1], tmp[:, J - 1::-1], ccol[:, :], ALU.mult, ALU.add))
                    ch.link(v.tensor_tensor(endpos[:, :], pos[:, :], cnt, ALU.subtract))
                    ch.link(v.tensor_tensor(endpos[:, :], endpos[:, :], degrow[:, :], ALU.add))

                    def chunk(i, q, first=False):
                        c = i * 2 + q
                        if not first:
                            dve.wait_ge(sent[q], i * (16 * C))
                        row = slots[q][:, 0:2 * C].rearrange("p (j t) -> p j t", t=2)
                        ch.tick(copy(nc, row[:, :, 0], cols(pos, c)))
                        ch.tick(v.tensor_copy(row[:, :, 1], cols(degrow, c)))
                        v.tensor_copy(islots[q][:, 0:C], cols(sidxS, c)).then_inc(filled, 1)

                    chunk(0, 0, True)
                    chunk(0, 1, True)
                    dense_dve(dve, ch, ds_, din, dout, dtmp, small)
                    with ch.loop(1, HALF, 4) as i:
                        chunk(i, 0)
                        chunk(i, 1)

        bn = ExitStack()
        W1bd, W2bd = sb(bn, "W1bd", [P, 2 * D]), sb(bn, "W2bd", [P, P])
        tT = sb(bn, "tT", [P, (C // 2) * P])
        psT = ps(bn, "psT", [P, 4 * 512])
        psH = ps(bn, "psH", [P, 2 * 512])
        with ExitStack() as ctx:
            taken, step5, wz, wl, flipped, tcopied, multiplied, used = (sem(ctx, n) for n in (
                "taken5", "dve_5", "wz5", "wl5", "flipped5", "tcopied5", "mult5", "used5"))
            staged = [sem(ctx, f"staged{q}_5") for q in range(2)]
            got = [sem(ctx, f"got{q}_5") for q in range(2)]
            with nc.Block() as block:
                @block.gpsimd
                def _(pool):
                    gather_pass(pool, staged, got, (T1, T1), D, MAXROW)

                @block.sync
                def _(sp):
                    sp.wait_ge(wz, 2)
                    for a in range(2):
                        sp.dma_start(W1bd[a * 2 * D:(a + 1) * 2 * D, a * D:(a + 1) * D], W1).then_inc(wl, 16)
                    for a in range(4):
                        sp.dma_start(W2bd[a * D:(a + 1) * D, a * D:(a + 1) * D], W2).then_inc(wl, 16)
                    stage_indices(sp, taken, staged, (srcS, dstS))

                @block.tensor
                def _(pe):
                    pe.wait_ge(wl, 16 * 6)
                    with pe.Fori(0, HALF) as i:
                        for q in range(2):
                            c = i * 2 + q
                            pe.wait_ge(got[q], i * (32 * C) + 32 * C)
                            pe.wait_ge(tcopied, c + 1)
                            for m in range(C // 2):
                                last = nc.tensor.transpose(psT[:, m * P:(m + 1) * P], slots[q][:, m * P:(m + 1) * P], ident[:, :])
                            last.then_inc(flipped, 1)
                            pe.wait_ge(tcopied, c + 2)
                            pe.wait_ge(used, c + 1)
                            for m in range(C // 2):
                                last = nc.tensor.matmul(psH[:, m * 2 * D:(m + 1) * 2 * D], tT[:, m * P:(m + 1) * P],
                                                        W1bd[:, :], start=True, stop=True)
                            last.then_inc(multiplied, 1)

                @block.scalar
                def _(act):
                    act.sem_inc(tcopied, 1)
                    with act.Fori(0, NCH) as c:
                        act.wait_ge(flipped, c + 1)
                        act.wait_ge(multiplied, c + 0) if False else None
                        nc.scalar.activation(tT[:, :], psT[:, 0:(C // 2) * P], ACT.Copy).then_inc(tcopied, 1)

                @block.vector
                def _(dve):
                    v = nc.vector
                    ch = Chain(dve, step5)
                    v.memset(W1bd[:, :], 0.0).then_inc(wz, 1)
                    v.memset(W2bd[:, :], 0.0).then_inc(wz, 1)
                    dve.sem_inc(taken, 2)
                    dve.sem_inc(used, 1)
                    with ch.loop(0, HALF, 4) as i:
                        for q in range(2):
                            c = i * 2 + q
                            dve.wait_ge(got[q], i * (32 * C) + 32 * C)
                            both = slots[q][:, :].rearrange("p (j t f) -> p j t f", t=2, f=D)
                            ch.link(copy(nc, rows3(cols(R2, c, D)), both[:, :, 0, :]))
                            dve.wait_ge(multiplied, c + 1)
                            h = rows3(cols(R1, c, D))
                            ch.link(v.tensor_tensor(h, rows3(psH[:, 0:CD]), repeat(b1v, C), ALU.add))
                            v.tensor_tensor(h, h, spread(cols(valid, c)), ALU.mult).then_inc(used, 1)
                            dve.sem_inc(taken, 1)

        with ExitStack() as ctx:
            part = sb(ctx, "part6", [P, D])
            mean, gm, vr = (sb(ctx, n, [P, D]) for n in ("mean6", "gm6", "vr6"))
            hn = sb(ctx, "hn6", [P, CD])
            eps6 = sb(ctx, "eps6", [P, 1])
            pss = [ps(ctx, "pssum", [P, D])]
            pst = ps(ctx, "pst6", [P, P])
            psb = pst
            cs = chain_sems(ctx, "6")
            step6, summed, total, rooted, asked, relued, flipped, tcopied, multiplied, hready = (sem(ctx, n) for n in (
                "dve_6", "summed6", "total6", "rooted6", "asked6", "relued6", "flipped6", "tcopied6", "mult6", "hready6"))
            NG = C // 4
            staged = [sem(ctx, f"staged{q}_6") for q in range(2)]
            copied = [sem(ctx, f"copied{q}_6") for q in range(2)]
            got = [sem(ctx, f"got{q}_6") for q in range(2)]
            with nc.Block() as block:
                @block.gpsimd
                def _(pool):
                    gather_pass(pool, staged, got, (NT,), 2, MAXROW)

                @block.sync
                def _(sp):
                    def indices(c, q):
                        sp.dma_start(islots[q][:, 0:C], cols(dstS, c)).then_inc(staged[q], 16)

                    def keep(i, q):
                        sp.wait_ge(got[q], i * (16 * C) + 16 * C)
                        sp.dma_start(cols(PD, i * 2 + q, 2), slots[q][:, 0:2 * C]).then_inc(copied[q], 16)
                        sp.wait_ge(copied[q], i * 16 + 16)

                    indices(0, 0)
                    indices(1, 1)
                    with sp.Fori(0, HALF - 1) as i:
                        for q in range(2):
                            keep(i, q)
                            indices(i * 2 + q + 2, q)
                    keep(HALF - 1, 0)
                    keep(HALF - 1, 1)

                @block.tensor
                def _(pe):
                    def totals(n):
                        pe.wait_ge(summed, n + 1)
                        nc.tensor.matmul(pss[0][:, :], ones[:, :], part[:, :], start=True, stop=True).then_inc(total, 1)
                    totals(0)
                    totals(1)
                    with pe.Fori(0, NCH) as c:
                        pe.wait_ge(relued, c + 1)
                        for m in range(NG):
                            last = nc.tensor.transpose(psT[:, m * P:(m + 1) * P], hn[:, m * P:(m + 1) * P], ident[:, :])
                        last.then_inc(flipped, 1)
                        pe.wait_ge(tcopied, c + 1)
                        for m in range(NG):
                            last = nc.tensor.matmul(psH[:, m * P:(m + 1) * P], tT[:, m * P:(m + 1) * P], W2bd[:, :],
                                                    start=True, stop=True)
                        last.then_inc(multiplied, 1)
                    totals(2)
                    totals(3)
                    carries_pe(pe, cs, 0, D, R3[:, J * D:(J + 1) * D], pst, psb)

                @block.scalar
                def _(act):
                    act.wait_ge(asked, 1)
                    nc.scalar.activation(vr[:, :], vr[:, :], ACT.Sqrt, bias=eps6[:, :], scale=1.0 / E).then_inc(rooted, 1)
                    with act.Fori(0, NCH) as c:
                        act.wait_ge(hready, c + 1)
                        nc.scalar.activation(hn[:, :], hn[:, :], ACT.Relu).then_inc(relued, 1)
                        act.wait_ge(flipped, c + 1)
                        nc.scalar.activation(tT[:, 0:NG * P], psT[:, 0:NG * P], ACT.Copy).then_inc(tcopied, 1)
                    act.wait_ge(asked, 2)
                    nc.scalar.activation(vr[:, :], vr[:, :], ACT.Sqrt, bias=eps6[:, :], scale=1.0 / E).then_inc(rooted, 1)

                @block.vector
                def _(dve):
                    v = nc.vector
                    ch = Chain(dve, step6)
                    ch.link(v.memset(eps6[:, :], BNEPS))
                    byfeature = R1[:, :].rearrange("p (j f) -> p f j", f=D)
                    R3b = R3[:, D:(J + 1) * D]

                    def stats(n, g):
                        ch.link(v.tensor_reduce(part[:, :], byfeature, AX, ALU.add))
                        dve.sem_inc(summed, 1)
                        dve.wait_ge(total, 2 * n + 1)
                        ch.link(v.tensor_scalar(mean[:, :], pss[0][:, :], 1.0 / E, None, ALU.mult))
                        ch.link(v.tensor_tensor(rows3(R1[:, :]), rows3(R1[:, :]), repeat(mean[:, :], J), ALU.subtract))
                        ch.link(v.tensor_tensor(rows3(R1[:, :]), rows3(R1[:, :]), spread(valid[:, :]), ALU.mult))
                        ch.link(v.tensor_tensor(R3b, R1[:, :], R1[:, :], ALU.mult))
                        ch.link(v.tensor_reduce(part[:, :], R3b.rearrange("p (j f) -> p f j", f=D), AX, ALU.add))
                        dve.sem_inc(summed, 1)
                        dve.wait_ge(total, 2 * n + 2)
                        ch.link(v.tensor_copy(vr[:, :], pss[0][:, :]))
                        dve.sem_inc(asked, 1)
                        dve.wait_ge(rooted, n + 1)
                        ch.link(v.reciprocal(gm[:, :], vr[:, :]))
                        ch.link(v.tensor_tensor(gm[:, :], gm[:, :], g, ALU.mult))

                    stats(0, g1v)
                    with ch.loop(0, NCH, 2) as c:
                        h = rows3(cols(R1, c, D))
                        ch.link(v.tensor_tensor(rows3(hn[:, :]), h, repeat(gm[:, :], C), ALU.mult))
                        v.tensor_tensor(rows3(hn[:, :]), rows3(hn[:, :]), repeat(be1v, C), ALU.add).then_inc(hready, 1)
                        dve.wait_ge(multiplied, c + 1)
                        ch.link(v.tensor_tensor(h, rows3(psH[:, 0:CD]), repeat(b2v, C), ALU.add))
                    ch.link(v.tensor_tensor(rows3(R1[:, :]), rows3(R1[:, :]), spread(valid[:, :]), ALU.mult))
                    stats(1, g2v)
                    ch.link(v.tensor_tensor(rows3(R1[:, :]), rows3(R1[:, :]), repeat(gm[:, :], J), ALU.mult))
                    ch.link(v.tensor_tensor(rows3(R1[:, :]), rows3(R1[:, :]), repeat(be2v, J), ALU.add))
                    ch.link(v.tensor_scalar(R1[:, :], R1[:, :], 0.0, None, ALU.max))
                    feature_scan(ch, contS, R1, R3)
                    dve.sem_inc(cs[0], 1)
                    carries_dve(ch, cs, 0, D, ATS, pst, psb, carry[:, :], ALU.mult, ALU.add, 0.0)
        bn.close()

        finish("l1", R2, R3, FS, sidxS, T2, keep=True)

        recycle()
        wS = valid
        nbi = sb(ordS, "nbi", [1, 1], I32)
        cpe = sb(ordS, "cpe", [P, J])
        with ExitStack() as ctx:
            live, c_, ct, g_, t_, wb, lp = (R1[:, n * J:(n + 1) * J] for n in range(7))
            idxi = R1[:, 7 * J:8 * J].bitcast(I32)
            zeros = R1[:, 8 * J:8 * J + CD]
            ccol, brow, kcol, jc, rj, over = (sb(ctx, n + "8", [P, 1]) for n in ("ccol", "brow", "kcol", "jc", "rj", "over"))
            ji = sb(ctx, "ji8", [P, 1], I32)
            qi = sb(ctx, "qi8", [P, J], I32)
            tri = sb(ctx, "tri8", [P, P])
            eps1 = sb(ctx, "eps8", [P, 1])
            pst, psb = ps(ctx, "pst8", [P, P]), ps(ctx, "psb8", [P, D])
            psk = ps(ctx, "psk8", [P, 2])
            cs = chain_sems(ctx, "8")
            step8, asked, rooted, filled, mask_made, counted, totals, put, zd = (sem(ctx, n + "8") for n in (
                "dve_", "asked", "rooted", "filled", "mask", "counted", "totals", "put", "zd"))
            sent = [sem(ctx, f"sent{q}_8") for q in range(2)]
            with dense_buffers(ctx, "t3") as (din, dout, dtmp, small, ds_), nc.Block() as block:
                @block.gpsimd
                def _(pool):
                    nc.gpsimd.memset(tri[:, :], 1.0).then_inc(mask_made, 1)
                    pool.wait_ge(mask_made, 1)
                    nc.gpsimd.affine_select(out=tri[:, :], in_=tri[:, :], compare_op=ALU.is_gt, fill=0.0,
                                            base=0, pattern=[[1, P]], channel_multiplier=-1).then_inc(mask_made, 1)
                    scatter_pass(pool, filled, sent, LIVE, 4)

                @block.sync
                def _(sp):
                    sp.dma_start(X2, R2[:, :]).then_inc(put, 16)
                    sp.wait_ge(zd, 1)
                    LSv = LS.rearrange("(p j) f -> p (j f)", p=P)
                    ULz = UL[0:EP, :].rearrange("(p j) f -> p (j f)", p=P)
                    with sp.Fori(0, NCH) as c:
                        for table in (LSv, ULz):
                            sp.dma_start(table[:, bass.ds(c * CD, CD)], zeros).then_inc(put, 16)
                    sp.wait_ge(put, 16 * (2 * NCH + 1))

                @block.scalar
                def _(act):
                    act.wait_ge(asked, 1)
                    nc.scalar.activation(t_, t_, ACT.Sqrt).then_inc(rooted, 1)
                    act.wait_ge(step8, 1)
                    dense_act(act, eps1, T2, T3, ds_, din, dout, dtmp)

                @block.tensor
                def _(pe):
                    carries_pe(pe, cs, 0, 1, c_[:, J - 1:J], pst, psb)
                    carries_pe(pe, cs, 1, 1, t_[:, 0:1], pst, psb, backward=True)
                    pe.wait_ge(mask_made, 2)
                    pe.wait_ge(counted, 1)
                    nc.tensor.matmul(psk[:, 0:1], tri[:, :], g_[:, J - 1:J], start=True, stop=True)
                    nc.tensor.matmul(psk[:, 1:2], ones[:, :], g_[:, J - 1:J], start=True, stop=True).then_inc(totals, 1)

                @block.vector
                def _(dve):
                    v = nc.vector
                    ch = Chain(dve, step8)
                    pd = PD[:, :].rearrange("p (j t) -> p j t", t=2)
                    ch.link(v.memset(eps1[:, :], LNEPS / (1.0 + ALPHA / GAMMA) ** 2))
                    v.memset(zeros, 0.0).then_inc(zd, 1)
                    ch.link(v.tensor_scalar(t_, degrow[:, :], 1.0, None, ALU.max))
                    ch.link(v.tensor_tensor(t_, t_, pd[:, :, 1], ALU.mult))
                    ch.link(v.tensor_scalar(t_, t_, 1.0, None, ALU.max))
                    dve.sem_inc(asked, 1)
                    ch.link(v.tensor_scalar(live, pd[:, :, 0], float(EP), None, ALU.is_lt))
                    ch.link(v.tensor_tensor(live, live, valid[:, :], ALU.mult))
                    dve.wait_ge(rooted, 1)
                    ch.link(v.reciprocal(t_, t_))
                    ch.link(v.tensor_tensor(wS[:, :], valid[:, :], t_, ALU.mult))
                    ch.link(v.tensor_scalar(wb, wS[:, :], BETA, None, ALU.mult))
                    ch.link(v.tensor_tensor_scan(c_, contS[:, :], live, 0.0, ALU.mult, ALU.add))
                    dve.sem_inc(cs[0], 1)
                    carries_dve(ch, cs, 0, 1, ATS, pst, psb, ccol[:, :], ALU.mult, ALU.add, 0.0)
                    ch.link(v.tensor_tensor_scan(c_, contS[:, :], live, ccol[:, :], ALU.mult, ALU.add))
                    ch.link(v.tensor_scalar(g_, nendS[:, :], -1.0, 1.0, ALU.mult, ALU.add))
                    ch.link(v.tensor_tensor(g_, g_, c_, ALU.mult))
                    ch.link(v.tensor_tensor_scan(t_[:, J - 1::-1], nendS[:, J - 1::-1], g_[:, J - 1::-1], 0.0, ALU.mult, ALU.add))
                    dve.sem_inc(cs[0], 1)
                    carries_dve(ch, cs, 1, 1, ABS, pst, psb, ccol[:, :], ALU.mult, ALU.add, 0.0, backward=True)
                    ch.link(v.tensor_tensor_scan(ct[:, J - 1::-1], nendS[:, J - 1::-1], g_[:, J - 1::-1], ccol[:, :], ALU.mult, ALU.add))
                    ch.link(v.tensor_tensor_scan(g_, live, live, 0.0, ALU.add, ALU.max))
                    dve.sem_inc(counted, 1)
                    dve.wait_ge(totals, 1)
                    ch.link(v.tensor_copy(ccol[:, :], psk[:, 0:1]))
                    ch.link(v.tensor_copy(kcol[:, :], psk[:, 1:2]))
                    ch.link(v.tensor_scalar(g_, g_, ccol[:, :], -1.0, ALU.add, ALU.add))

                    def ceil_div(out_, n, d):
                        ch.link(v.tensor_scalar(kcol[:, :], n, float(d - 1), 1.0 / d, ALU.add, ALU.mult))
                        ch.link(v.tensor_copy(ji[:, :], kcol[:, :]))
                        ch.link(v.tensor_copy(out_, ji[:, :]))
                        ch.link(v.tensor_tensor(over[:, :], out_, kcol[:, :], ALU.is_gt))
                        ch.link(v.tensor_tensor(out_, out_, over[:, :], ALU.subtract))
                        ch.link(v.tensor_scalar(out_, out_, 1.0, None, ALU.max))

                    ceil_div(jc[:, :], kcol[:, :], P)
                    ch.link(v.memset(rj[:, :], 0.0))
                    for n in range(HALF):
                        ch.link(v.tensor_scalar(over[:, :], jc[:, :], float(2 * C * n), None, ALU.is_gt))
                        ch.link(v.tensor_tensor(rj[:, :], rj[:, :], over[:, :], ALU.add))
                    ch.link(v.tensor_scalar(rj[:, :], rj[:, :], 2.0, None, ALU.max))
                    ch.link(v.tensor_copy(nbi[:, :], rj[0:1, :]))
                    ch.link(v.reciprocal(rj[:, :], jc[:, :]))
                    ch.link(v.tensor_scalar(t_, g_, rj[:, :], None, ALU.mult))
                    ch.link(v.tensor_copy(qi[:, :], t_))
                    q_ = cpe[:, :]
                    ch.link(v.tensor_copy(q_, qi[:, :]))
                    for _ in range(1):
                        ch.link(v.tensor_scalar(t_, q_, jc[:, :], None, ALU.mult))
                        ch.link(v.tensor_tensor(t_, g_, t_, ALU.subtract))
                        ch.link(v.tensor_scalar(lp, t_, jc[:, :], None, ALU.is_ge))
                        ch.link(v.tensor_tensor(q_, q_, lp, ALU.add))
                        ch.link(v.tensor_scalar(lp, t_, 0.0, None, ALU.is_lt))
                        ch.link(v.tensor_tensor(q_, q_, lp, ALU.subtract))
                    ch.link(v.tensor_scalar(rj[:, :], jc[:, :], -1.0, float(J), ALU.mult, ALU.add))
                    ch.link(v.tensor_scalar(t_, q_, rj[:, :], None, ALU.mult))
                    ch.link(v.tensor_tensor(g_, g_, t_, ALU.add))
                    ch.link(v.tensor_scalar(t_, c_, 0.0, None, ALU.is_gt))
                    ch.link(v.tensor_scalar(cpe[:, :], g_, -float(EP), None, ALU.add))
                    ch.link(v.tensor_tensor(cpe[:, :], cpe[:, :], t_, ALU.mult))
                    ch.link(v.tensor_scalar(cpe[:, :], cpe[:, :], float(EP), None, ALU.add))
                    ch.link(v.tensor_tensor(lp, c_, ct, ALU.is_equal))
                    ch.link(v.tensor_scalar(t_, endpos[:, :], -float(N), None, ALU.add))
                    ch.link(v.tensor_tensor(lp, lp, t_, ALU.mult))
                    ch.link(v.tensor_scalar(lp, lp, float(N), None, ALU.add))
                    ch.link(v.tensor_scalar(c_, c_, 2.0, None, ALU.is_ge))
                    ch.link(v.tensor_scalar(g_, g_, -float(N), None, ALU.add))
                    ch.link(v.tensor_tensor(g_, g_, live, ALU.mult))
                    ch.link(v.tensor_scalar(g_, g_, float(N), None, ALU.add))
                    ch.link(v.tensor_copy(idxi, g_))

                    def chunk(i, q, first=False):
                        c = i * 2 + q
                        if not first:
                            dve.wait_ge(sent[q], i * (16 * C))
                        row = slots[q][:, 0:4 * C].rearrange("p (j t) -> p j t", t=4)
                        ch.tick(copy(nc, row[:, :, 0], PD[:, bass.ds(c * (2 * C), C, step=2)]))
                        ch.tick(v.tensor_copy(row[:, :, 1], cols(wb, c)))
                        ch.tick(v.tensor_copy(row[:, :, 2], cols(c_, c)))
                        ch.tick(v.tensor_copy(row[:, :, 3], cols(lp, c)))
                        v.tensor_copy(islots[q][:, 0:C], cols(idxi, c)).then_inc(filled, 1)

                    chunk(0, 0, True)
                    chunk(0, 1, True)
                    dense_dve(dve, ch, ds_, din, dout, dtmp, small)
                    with ch.loop(1, HALF, 8) as i:
                        chunk(i, 0)
                        chunk(i, 1)

        with ExitStack() as ctx:
            m = sb(ctx, "m9", [P, CD])
            pst, psb = ps(ctx, "pst9", [P, P]), ps(ctx, "psb9", [P, D])
            taken, step9, fixed = sem(ctx, "taken9"), sem(ctx, "dve_9"), sem(ctx, "fixed9")
            staged = [sem(ctx, f"staged{q}_9") for q in range(2)]
            got = [sem(ctx, f"got{q}_9") for q in range(2)]
            put = [sem(ctx, f"put{q}_9") for q in range(2)]
            cs = chain_sems(ctx, "9")
            Uv = U[0:EP, :].rearrange("(p j) f -> p (j f)", p=P)
            with nc.Block() as block:
                @block.gpsimd
                def _(pool):
                    gather_pass(pool, staged, got, (T2,), D, MAXROW)

                @block.sync
                def _(sp):
                    stage_indices(sp, taken, staged, (dstS,))
                    with sp.Fori(0, HALF) as i:
                        for q in range(2):
                            c = i * 2 + q
                            sp.wait_ge(fixed, c + 1)
                            sp.dma_start(Uv[:, bass.ds(c * (C * UW), C * UW)], slots[q][:, 0:C * UW]).then_inc(put[q], 16)
                    for q in range(2):
                        sp.wait_ge(put[q], 16 * HALF)

                @block.tensor
                def _(pe):
                    carries_pe(pe, cs, 0, D, R3[:, J * D:(J + 1) * D], pst, psb)

                @block.vector
                def _(dve):
                    v = nc.vector
                    ch = Chain(dve, step9)
                    dve.sem_inc(taken, 2)
                    ch.link(v.memset(R3[:, 0:D], 0.0))
                    with ch.loop(0, HALF, 2 * (1 + D)) as i:
                        for q in range(2):
                            c = i * 2 + q
                            dve.wait_ge(got[q], i * (16 * C) + 16 * C)
                            ch.link(v.tensor_tensor(rows3(m[:, :]), rows3(slots[q][:, 0:CD]), spread(cols(wS, c)), ALU.mult))
                            dve.sem_inc(taken, 1)
                            for f in range(D):
                                ch.tick(v.tensor_tensor_scan(
                                    R3[:, bass.ds(c * CD + D + f, C, step=D)], cols(contS, c),
                                    m[:, f:f + (C - 1) * D + 1:D], R3[:, bass.ds(c * CD + f, 1)], ALU.mult, ALU.add))
                            dve.wait_ge(ch.sem, ch.value())
                    dve.sem_inc(cs[0], 1)
                    carries_dve(ch, cs, 0, D, ATS, pst, psb, carry[:, :], ALU.mult, ALU.add, 0.0)

                    def fix(i, q, first=False):
                        c = i * 2 + q
                        s3 = R3[:, bass.ds(c * CD + D, CD)]
                        ch.link(v.tensor_tensor(rows3(m[:, :]), spread(cols(FS, c)), repeat(carry[:, :], C), ALU.mult))
                        ch.link(v.tensor_tensor(s3, s3, m[:, :], ALU.add))
                        if not first:
                            dve.wait_ge(put[q], i * 16)
                        row = slots[q][:, 0:C * UW].rearrange("p (j t) -> p j t", t=UW)
                        ch.tick(copy(nc, row[:, :, 0:D], rows3(s3)))
                        v.tensor_copy(row[:, :, D], cols(cpe, c)).then_inc(fixed, 1)

                    fix(0, 0, True)
                    fix(0, 1, True)
                    with ch.loop(1, HALF, 6) as i:
                        fix(i, 0)
                        fix(i, 1)

        with ExitStack() as ctx:
            m = sb(ctx, "m10", [P, CD])
            last = sb(ctx, "last10", [P, D])
            tab = sb(ctx, "tab10", [P, J * 4])
            FL = nendS
            ATL, arep = sb(ctx, "ATL", [D, P]), last
            iseg = srcS
            iplace, iback = dstS, endpos[:, :].bitcast(I32)
            RL = R2
            pst, psb = ps(ctx, "pst10", [P, P]), ps(ctx, "psb10", [P, D])
            tabd, taken, step10, fixed, stored, listed, filled, at_ready, ar, loops = (sem(ctx, n + "10") for n in (
                "tabd", "taken", "dve_", "fixed", "stored", "listed", "filled", "at_ready", "arep_ready", "loops"))
            staged = [sem(ctx, f"staged{q}_10") for q in range(2)]
            got = [sem(ctx, f"got{q}_10") for q in range(2)]
            sent = [sem(ctx, f"sent{q}_10") for q in range(2)]
            cs = chain_sems(ctx, "10")
            LOOPS = KSTEPS - 2
            ULv = UL[0:EP, :].rearrange("(p j) f -> p (j f)", p=P)

            def tcol(n, c):
                return tab[:, bass.ds(c * (4 * C) + n, C, step=4)]

            with nc.Block() as block:
                @block.gpsimd
                def _(pool):
                    nb = pool.value_load(nbi[0:1, 0:1], min_val=2, max_val=HALF)
                    limit = pool.to_reg(EP)
                    with pool.Fori(0, nb) as i:
                        for q in range(2):
                            pool.wait_ge(staged[q], i * 16 + 16)
                            pool.sem_inc(begun, 1)
                            gather(pool, i, q, got, (U,), UW, limit)
                    with pool.Fori(1, LOOPS + 1) as t:
                        pool.wait_ge(stored, t * nb * 32)
                        pool.sem_inc(begun, 1)
                        with pool.Fori(0, nb) as i:
                            for q in range(2):
                                pool.wait_ge(staged[q], t * nb * 16 + i * 16 + 16)
                                pool.sem_inc(begun, 1)
                                gather(pool, i, q, got, (UL,), D, limit)
                    backlimit = pool.to_reg(EP - 1)
                    with pool.Fori(0, nb) as i:
                        for q in range(2):
                            pool.wait_ge(filled, i * 2 + q + 1)
                            pool.sem_inc(begun, 1)
                            for j in range(C):
                                pool.indirect_dma_start(LS, bass.IndirectOffsetOnAxis(ap=islots[q][:, j:j + 1], axis=0),
                                                        slots[q][:, j * D:(j + 1) * D], None,
                                                        bounds_check=backlimit, oob_is_err=False).then_inc(sent[q], 16)
                    for q in range(2):
                        pool.wait_ge(sent[q], nb * (16 * C))

                @block.sync
                def _(sp):
                    sp.dma_start(tab[:, :], LIVE.rearrange("(p n) t -> p (n t)", p=P)).then_inc(tabd, 16)
                    nb = sp.value_load(nbi[0:1, 0:1], min_val=2, max_val=HALF)
                    sp.wait_ge(listed, 1)
                    with sp.Fori(0, nb) as i:
                        for q in range(2):
                            sp.wait_ge(taken, i * 2 + q + 1)
                            sp.dma_start(islots[q][:, 0:C], cols(iseg, i * 2 + q)).then_inc(staged[q], 16)
                    with sp.Fori(1, LOOPS + 1) as t:
                        with sp.Fori(0, nb) as i:
                            for q in range(2):
                                c = i * 2 + q
                                sp.wait_ge(fixed, (t - 1) * nb * 2 + c + 1)
                                sp.dma_start(ULv[:, bass.ds(c * CD, CD)], cols(RL, c, D)).then_inc(stored, 16)
                        with sp.Fori(0, nb) as i:
                            for q in range(2):
                                sp.wait_ge(taken, t * nb * 2 + i * 2 + q + 1)
                                sp.dma_start(islots[q][:, 0:C], cols(iplace, i * 2 + q)).then_inc(staged[q], 16)

                @block.tensor
                def _(pe):
                    pe.wait_ge(ar, 1)
                    nc.tensor.transpose(pst[0:D, :], arep[:, :], ident[:, :]).then_inc(at_ready, 1)
                    with pe.Fori(0, LOOPS + 1) as t:
                        carries_pe(pe, cs, t, D, last[:, :], pst, psb)

                @block.vector
                def _(dve):
                    v = nc.vector
                    ch = Chain(dve, step10)
                    nb = dve.value_load(nbi[0:1, 0:1], min_val=2, max_val=HALF)
                    tt = tab[:, :].rearrange("p (j t) -> p j t", t=4)
                    dve.wait_ge(tabd, 16)
                    ch.link(v.tensor_copy(iseg[:, :], tt[:, :, 0]))
                    ch.link(v.tensor_copy(iback, tt[:, :, 3]))
                    dve.sem_inc(listed, 1)
                    dve.sem_inc(taken, 2)
                    ch.link(v.tensor_tensor_scan(FL[:, :], tt[:, :, 2], tt[:, :, 2], 1.0, ALU.mult, ALU.min))
                    ch.link(v.tensor_copy(arep[:, :], FL[:, J - 1:J].broadcast_to([P, D])))
                    dve.sem_inc(ar, 1)
                    dve.wait_ge(at_ready, 1)
                    ch.link(v.tensor_copy(ATL[:, :], pst[0:D, :]))
                    ch.link(v.memset(last[:, :], 0.0))

                    def sums(ch, c):
                        for f in range(D):
                            ch.tick(v.tensor_tensor_scan(
                                RL[:, bass.ds(c * CD + f, C, step=D)], tcol(2, c),
                                m[:, f:f + (C - 1) * D + 1:D], last[:, f:f + 1], ALU.mult, ALU.add))
                        dve.wait_ge(ch.sem, ch.value())
                        ch.link(v.tensor_copy(last[:, :], RL[:, bass.ds(c * CD + CD - D, D)]))

                    with ch.loop(0, nb, 2 * (3 + D + 1)) as i:
                        for q in range(2):
                            c = i * 2 + q
                            dve.wait_ge(got[q], i * (16 * C) + 16 * C)
                            row = slots[q][:, 0:C * UW].rearrange("p (j t) -> p j t", t=UW)
                            ch.link(v.tensor_tensor(rows3(m[:, :]), row[:, :, 0:D], spread1(tcol(1, c)), ALU.mult))
                            ch.link(v.tensor_copy(cols(iplace, c), row[:, :, D]))
                            dve.sem_inc(taken, 1)
                            ch.link(v.tensor_scalar(cols(R1, c, D), m[:, :], ALPHA, None, ALU.mult))
                            sums(ch, c)
                    dve.sem_inc(cs[0], 1)
                    carries_dve(ch, cs, 0, D, ATL, pst, psb, carry[:, :], ALU.mult, ALU.add, 0.0)
                    dve.sem_inc(loops, 1)
                    with ch.loop(1, LOOPS + 1, nb * (2 + 2 * (3 + D)) + 3, nested=True) as t:
                        ch.link(v.memset(last[:, :], 0.0))
                        dve.sem_inc(loops, 1)
                        with ch.loop(0, nb, 2) as i:
                            for q in range(2):
                                c = i * 2 + q
                                ch.link(v.tensor_tensor(rows3(m[:, :]), spread(cols(FL, c)), repeat(carry[:, :], C), ALU.mult))
                                v.tensor_tensor(cols(RL, c, D), cols(RL, c, D), m[:, :], ALU.add).then_inc(fixed, 1)
                                dve.wait_ge(fixed, (t - 1) * nb * 2 + c + 1)
                        dve.sem_inc(loops, 1)
                        with ch.loop(0, nb, 2 * (2 + D + 1)) as i:
                            for q in range(2):
                                c = i * 2 + q
                                dve.wait_ge(got[q], t * nb * (16 * C) + i * (16 * C) + 16 * C)
                                ch.link(v.tensor_tensor(rows3(m[:, :]), rows3(slots[q][:, 0:CD]), spread1(tcol(1, c)), ALU.mult))
                                dve.sem_inc(taken, 1)
                                ch.link(v.tensor_tensor(m[:, :], m[:, :], cols(R1, c, D), ALU.add))
                                sums(ch, c)
                        dve.sem_inc(cs[0], 1)
                        carries_dve(ch, cs, t, D, ATL, pst, psb, carry[:, :], ALU.mult, ALU.add, 0.0)

                    def back(i, q, first=False):
                        c = i * 2 + q
                        ch.link(v.tensor_tensor(rows3(m[:, :]), spread(cols(FL, c)), repeat(carry[:, :], C), ALU.mult))
                        if not first:
                            dve.wait_ge(sent[q], i * (16 * C))
                        ch.link(v.tensor_tensor(slots[q][:, 0:CD], cols(RL, c, D), m[:, :], ALU.add))
                        v.tensor_copy(islots[q][:, 0:C], cols(iback, c)).then_inc(filled, 1)

                    back(0, 0, True)
                    back(0, 1, True)
                    dve.sem_inc(loops, 1)
                    with ch.loop(1, nb, 4) as i:
                        back(i, 0)
                        back(i, 1)

        with ExitStack() as ctx:
            reload_ = sem(ctx, "reload11")
            with nc.Block() as block:
                @block.sync
                def _(sp):
                    sp.dma_start(R2[:, :], X2).then_inc(reload_, 16)
                    sp.dma_start(R1[:, :], LS.rearrange("(p j) f -> p (j f)", p=P)).then_inc(reload_, 16)
                    sp.wait_ge(reload_, 32)

        finish("l2", R2, R3, FS, sidxS, T3, plus=R1, own_scale=1.0 + ALPHA / GAMMA, sum_scale=BETA / GAMMA)
        ordS.close()

        recycle()
        with ExitStack() as ctx:
            eps1 = sb(ctx, "eps12", [P, 1])
            step12 = sem(ctx, "dve_12")
            staged = [sem(ctx, f"staged{q}_12") for q in range(2)]
            got = [sem(ctx, f"got{q}_12") for q in range(2)]
            with dense_buffers(ctx, "o") as (din, dout, dtmp, small, ds_), nc.Block() as block:
                @block.sync
                def _(sp):
                    for q in range(2):
                        sp.dma_start(islots[q][:, 0:C], cols(srcD, q)).then_inc(staged[q], 16)
                        sp.dma_start(islots[q][:, C:2 * C], cols(dstD, q)).then_inc(staged[q], 16)
                    for q in range(2):
                        sp.wait_ge(got[q], 32 * C)

                @block.gpsimd
                def _(pool):
                    limit = pool.to_reg(MAXROW)
                    for q in range(2):
                        pool.wait_ge(staged[q], 32)
                        gather(pool, 0, q, got, (T3, T3), D, limit)

                @block.scalar
                def _(act):
                    act.wait_ge(step12, 1)
                    dense_act(act, eps1, T3, out, ds_, din, dout, dtmp)

                @block.vector
                def _(dve):
                    ch = Chain(dve, step12)
                    ch.link(nc.vector.memset(eps1[:, :], LNEPS))
                    dense_dve(dve, ch, ds_, din, dout, dtmp, small)

        lay.close()

        with ExitStack() as ctx:
            r1, wt = sb(ctx, "r1", [P, J * 3]), sb(ctx, "wt", [P, J])
            mlp = sb(ctx, "mlp", [74, C * P])
            HT, emb = [mlp[0:32, :], mlp[32:64, :]], mlp[64:74, :]
            w1c, w2c = sb(ctx, "w1c", [74, 64]), sb(ctx, "w2c", [64, 896])
            sds = [sb(ctx, f"sds{q}", [P, C * 48]) for q in range(2)]
            v1s = [sb(ctx, f"v1s{q}", [P, C * 48]) for q in range(2)]
            vtmp = sb(ctx, "vtmp", [P, C * 16])
            prs = [sb(ctx, f"pr{b}", [P, 768]) for b in range(2)]
            prs2 = [sb(ctx, f"prs{b}", [P, 512]) for b in range(2)]
            T48, T64 = sb(ctx, "T48", [P, C * 48]), sb(ctx, "T64", [P, C * 64])
            sdsds, vtmp2 = sb(ctx, "sdsds", [P, C * 40]), sb(ctx, "vtmp2", [P, C * 8])
            vt = sb(ctx, "vt13", [P, C * 24])
            o16, th = sb(ctx, "o16", [P, 2 * C * 8]), sb(ctx, "th", [P, 2 * C * 8])
            n3, n3b = prs[0][:, 0:J], prs[1][:, 0:J]
            psHT = [ps(ctx, f"psHT{b}", [P, 512]) for b in range(2)]
            psw = [ps(ctx, f"psw{b}", [P, 512]) for b in range(2)]
            psx = [ps(ctx, f"psx{b}", [P, 512]) for b in range(2)]
            (taken, step13, loaded, asked, rooted, hid, hidd, embl, embf, w1r, w1u, w2r, w2u, sct, tanhed, pz, spread_) = (
                sem(ctx, n + "13") for n in ("taken", "dve_", "loaded", "asked", "rooted", "hid", "hidd", "embl",
                                             "embf", "w1r", "w1u", "w2r", "w2u", "sct", "tanhed", "pz", "spread"))
            staged = [sem(ctx, f"staged{q}_13") for q in range(2)]
            got = [sem(ctx, f"got{q}_13") for q in range(2)]
            G4 = C // 4
            assert G4 % 2 == 1
            C1 = float(32.0 ** -0.5 / 4.0)
            C2 = float(16.0 ** -0.5 / 4.0)
            SQRT3 = float(3.0 ** 0.5)
            with nc.Block() as block:
                @block.gpsimd
                def _(pool):
                    limit = pool.to_reg(MAXROW)
                    with pool.Fori(1, HALF) as i:
                        for q in range(2):
                            pool.wait_ge(staged[q], i * 32)
                            pool.sem_inc(begun, 1)
                            gather(pool, i, q, got, (T3, T3), D, limit)

                @block.sync
                def _(sp):
                    sp.dma_start(r1[:, :], attr3).then_inc(loaded, 16)
                    sp.dma_start(wt[:, :], weight).then_inc(loaded, 16)
                    sp.wait_ge(pz, 1)
                    sp.dma_start(w1c[64:74, 0:16], fc1_w1).then_inc(loaded, 16)
                    sp.dma_start(w1c[64:74, 16:32], fc2_w1).then_inc(loaded, 16)
                    for q in range(2):
                        sp.dma_start(w2c[32 * q:32 * q + 16, 0:512], fc1_w2).then_inc(loaded, 16)
                        sp.dma_start(w2c[32 * q + 16:32 * q + 32, 512:896], fc2_w2).then_inc(loaded, 16)
                    for c in range(2):
                        sp.wait_ge(embf, c + 1)
                        sp.dma_start(emb, attr10t[:, c * (C * P):(c + 1) * (C * P)]).then_inc(embl, 16)
                    with sp.Fori(1, HALF) as i:
                        for q in range(2):
                            c = i * 2 + q
                            sp.wait_ge(taken, c - 1)
                            sp.dma_start(islots[q][:, 0:C], cols(srcD, c)).then_inc(staged[q], 16)
                            sp.dma_start(islots[q][:, C:2 * C], cols(dstD, c)).then_inc(staged[q], 16)
                            sp.wait_ge(embf, c + 1)
                            sp.dma_start(emb, attr10t[:, bass.ds(c * (C * P), C * P)]).then_inc(embl, 16)

                @block.tensor
                def _(pe):
                    def hidden(c, q):
                        pe.wait_ge(embl, c * 16 + 16)
                        for g in range(G4):
                            pe.wait_ge(hidd, c * G4 + g + 1)
                            nc.tensor.matmul(psHT[(q + g) % 2][0:64, :], w1c[64:74, :], emb[:, g * 512:(g + 1) * 512],
                                             start=True, stop=True).then_inc(hid, 1)

                    def first(c, q, j):
                        if j == 0:
                            pe.wait_ge(hidd, c * G4 + G4 + 2)
                        pe.wait_ge(w1u, c * C + j + 1)
                        nc.tensor.matmul(psw[j % 2][:, :], HT[q][:, j * P:(j + 1) * P], w2c[32 * q:32 * q + 32, 0:512],
                                         start=True, stop=True).then_inc(w1r, 1)

                    def second(c, q, j):
                        pe.wait_ge(w2u, c * C + j + 1)
                        nc.tensor.matmul(psx[j % 2][:, 0:384], HT[q][:, j * P:(j + 1) * P],
                                         w2c[32 * q:32 * q + 32, 512:896], start=True, stop=True).then_inc(w2r, 1)

                    def both(c, q):
                        for j in range(C):
                            first(c + 1, 1 - q, j)
                            second(c, q, j)

                    pe.wait_ge(pz, 3)
                    hidden(0, 0)
                    hidden(1, 1)
                    for j in range(C):
                        first(0, 0, j)
                    with pe.Fori(0, HALF - 1) as i:
                        for q in range(2):
                            both(i * 2 + q, q)
                            hidden(i * 2 + q + 2, q)
                    both(NCH - 2, 0)
                    for j in range(C):
                        second(NCH - 1, 1, j)

                @block.scalar
                def _(act):
                    def hidden(c, q):
                        for g in range(G4):
                            act.wait_ge(hid, c * G4 + g + 1)
                            nc.scalar.activation(HT[q][:, g * 512:(g + 1) * 512], psHT[(q + g) % 2][0:32, :], ACT.Relu,
                                                 scale=float(10 ** -0.5)).then_inc(hidd, 1)
                        act.sem_inc(embf, 1)

                    def rows(i, q, begin=False):
                        if not begin:
                            act.wait_ge(got[q], i * (32 * C))
                            act.wait_ge(sct, i * 2 + q - 1)
                        both = slots[q][:, :].rearrange("p (j t f) -> p j t f", t=2, f=D)
                        s3 = sds[q][:, :].rearrange("p (j g t u) -> p j g t u", g=3, t=2, u=8)
                        v3 = v1s[q][:, :].rearrange("p (j k t u) -> p j k t u", k=3, t=2, u=8)
                        nc.scalar.activation(rows3(cols(R2, i * 2 + q, D)), both[:, :, 1, :], ACT.Copy).then_inc(spread_, 1)
                        for g in (0, 2):
                            nc.scalar.activation(s3[:, :, g], both[:, :, :, 0:8], ACT.Copy).then_inc(spread_, 1)
                        for k in range(3):
                            nc.scalar.activation(v3[:, :, k], both[:, :, :, 8 + k:32:3], ACT.Copy).then_inc(spread_, 1)
                        act.wait_ge(spread_, (i * 2 + q) * 6 + 6)
                        act.sem_inc(taken, 1)

                    def gates(c):
                        act.wait_ge(sct, c + 2)
                        nc.scalar.activation(th[:, :], o16[:, :], ACT.Tanh).then_inc(tanhed, 1)

                    act.wait_ge(asked, 1)
                    nc.scalar.activation(n3, n3, ACT.Sqrt).then_inc(rooted, 1)
                    hidden(0, 0)
                    hidden(1, 1)
                    rows(0, 0, begin=True)
                    rows(0, 1, begin=True)
                    with act.Fori(0, HALF - 1) as i:
                        for q in range(2):
                            rows(i + 1, q)
                            gates(i * 2 + q)
                            hidden(i * 2 + q + 2, q)
                    gates(NCH - 2)
                    gates(NCH - 1)

                @block.vector
                def _(dve):
                    v = nc.vector
                    ch = Chain(dve, step13)
                    ch.link(v.memset(w2c[:, :], 0.0))
                    v.memset(w1c[:, :], 0.0).then_inc(pz, 1)
                    dve.sem_inc(w1u, 2)
                    dve.sem_inc(w2u, 2)
                    dve.sem_inc(hidd, 2)
                    dve.sem_inc(embf, 1)
                    dve.wait_ge(loaded, 128)
                    v.tensor_scalar(w2c[:, 0:512], w2c[:, 0:512], C1, None, ALU.mult).then_inc(pz, 1)
                    v.tensor_scalar(w2c[:, 512:896], w2c[:, 512:896], C2, None, ALU.mult).then_inc(pz, 1)
                    r3 = r1[:, :].rearrange("p (j k) -> p j k", k=3)
                    ch.link(v.tensor_tensor(n3, r3[:, :, 0], r3[:, :, 0], ALU.mult))
                    for k in (1, 2):
                        ch.link(v.tensor_tensor(n3b, r3[:, :, k], r3[:, :, k], ALU.mult))
                        ch.link(v.tensor_tensor(n3, n3, n3b, ALU.add))
                    dve.sem_inc(asked, 1)
                    dve.wait_ge(rooted, 1)
                    ch.link(v.reciprocal(n3b, n3))
                    ch.link(v.tensor_tensor(r3, r3, spread(n3b, 3), ALU.mult))

                    def direction(c, k):
                        return r1[:, bass.ds(c * (3 * C) + k, C, step=3)]

                    def dot_r(c, parts, acc, tmp, n):
                        ch.link(v.tensor_tensor(acc, parts[0], spread(direction(c, 0), n), ALU.mult))
                        for k in (1, 2):
                            ch.link(v.tensor_tensor(tmp, parts[k], spread(direction(c, k), n), ALU.mult))
                            ch.link(v.tensor_tensor(acc, acc, tmp, ALU.add))

                    done = {}

                    def column(which, c, q, j):
                        ready, used, w, pj, n, u, mult, vectors, _ = of(which, q, j)
                        if j >= 2:
                            dve.wait_ge(ch.sem, done[which, j - 2])
                        dve.wait_ge(ready, c * C + j + 1)
                        m = n // 8
                        v.tensor_tensor(pj[:, 0:n].rearrange("p (a w) -> p a w", w=8),
                                        w[:, 0:n].rearrange("p (a w) -> p a w", w=8),
                                        spread(mult[:, j * m:(j + 1) * m], 8), ALU.mult)
                        wv = w[:, n:n + u * 8].rearrange("p (k u w) -> p k u w", k=1, w=8)
                        vj = vectors[:, j * 3 * u:(j + 1) * 3 * u].rearrange("p (k u b) -> p k u b", k=3, b=1)
                        v.tensor_tensor(pj[:, n:n + 3 * u * 8].rearrange("p (k u w) -> p k u w", k=3, w=8),
                                        wv.broadcast_to([P, 3, u, 8]), vj.broadcast_to([P, 3, u, 8]),
                                        ALU.mult).then_inc(used, 1)

                    def total(which, c, q, j):
                        _, used, _, pj, n, u, _, _, out_ = of(which, q, j)
                        dve.wait_ge(used, c * C + j + 3)
                        ch.tick(v.tensor_reduce(out_.rearrange("p (g w) -> p g w", w=8),
                                                pj[:, 0:n + 3 * u * 8].rearrange("p (g u w) -> p g w u", u=u, w=8),
                                                AX, ALU.add))
                        done[which, j] = ch.value()

                    def of(which, q, j):
                        if which == 1:
                            return (w1r, w1u, psw[j % 2], prs[j % 2], 384, 16, sds[q], v1s[q], T48[:, j * 48:(j + 1) * 48])
                        return w2r, w2u, psx[j % 2], prs2[j % 2], 320, 8, sdsds, vt, T64[:, j * 64:(j + 1) * 64]

                    def products(steps):
                        dve.wait_ge(ch.sem, ch.value())
                        before = None
                        for j in range(C):
                            for which, c, q in steps:
                                column(which, c, q, j)
                                if before:
                                    total(*before)
                                before = (which, c, q, j)
                        total(*before)
                        dve.wait_ge(ch.sem, ch.value())

                    t6 = T48[:, :].rearrange("p (j g w) -> p j g w", g=6, w=8)
                    t8 = T64[:, :].rearrange("p (j g w) -> p j g w", g=8, w=8)
                    vt3 = vt[:, :].rearrange("p (j k w) -> p j k w", k=3, w=8)
                    d5 = sdsds[:, :].rearrange("p (j g w) -> p j g w", g=5, w=8)
                    oo = o16[:, :].rearrange("p (a j w) -> p a j w", a=2, w=8)
                    tt = th[:, :].rearrange("p (a j w) -> p a j w", a=2, w=8)
                    t2 = rows3(vtmp2[:, :], 8)

                    def dots(c, q):
                        dve.wait_ge(spread_, c * 6 + 6)
                        v1j = v1s[q][:, :].rearrange("p (j k u) -> p j k u", k=3, u=16)
                        s3 = sds[q][:, :].rearrange("p (j g u) -> p j g u", g=3, u=16)
                        dot_r(c, [v1j[:, :, k] for k in range(3)], s3[:, :, 1], rows3(vtmp[:, :], 16), 16)

                    def between(c):
                        ch.tick(v.tensor_tensor(d5[:, :, 0], t6[:, :, 0], t6[:, :, 1], ALU.add))
                        for k in range(3):
                            ch.link(v.tensor_tensor(t2, t6[:, :, 2], spread(direction(c, k), 8), ALU.mult))
                            ch.link(v.scalar_tensor_tensor(vt3[:, :, k], t2, SQRT3, t6[:, :, 3 + k], ALU.mult, ALU.add))
                        dot_r(c, [vt3[:, :, k] for k in range(3)], d5[:, :, 1], t2, 8)
                        ch.tick(v.tensor_copy(d5[:, :, 2:5:2], d5[:, :, 0:1].broadcast_to([P, C, 2, 8])))
                        ch.tick(v.tensor_copy(d5[:, :, 3], d5[:, :, 1]))

                    def scalars(c):
                        ch.link(v.tensor_tensor(oo[:, 0], t8[:, :, 0], t8[:, :, 1], ALU.add))
                        v.tensor_tensor(oo[:, 1], t8[:, :, 2], t8[:, :, 3], ALU.add).then_inc(sct, 1)

                    def outputs(c):
                        dve.wait_ge(tanhed, c + 1)
                        eo = rows3(cols(R1, c, D))
                        wj = cols(wt, c)
                        ch.tick(v.tensor_tensor(eo[:, :, 0:8], tt[:, 0], spread(wj, 8), ALU.mult))
                        ch.link(v.tensor_tensor(tt[:, 1], tt[:, 1], spread(wj, 8), ALU.mult))
                        for k in range(3):
                            ch.link(v.tensor_tensor(t2, t8[:, :, 4], spread(direction(c, k), 8), ALU.mult))
                            ch.link(v.scalar_tensor_tensor(t2, t2, SQRT3, t8[:, :, 5 + k], ALU.mult, ALU.add))
                            ch.link(v.tensor_tensor(eo[:, :, 8 + k:32:3], t2, tt[:, 1], ALU.mult))

                    def step(c, q):
                        dots(c + 1, 1 - q)
                        products([(1, c + 1, 1 - q), (2, c, q)])
                        scalars(c)
                        between(c + 1)
                        outputs(c)

                    dots(0, 0)
                    products([(1, 0, 0)])
                    dve.sem_inc(sct, 1)
                    between(0)
                    with ch.loop(0, HALF - 1, 2 * (5 + 2 * C + 1 + 14 + 11)) as i:
                        step(i * 2, 0)
                        step(i * 2 + 1, 1)
                    step(NCH - 2, 0)
                    products([(2, NCH - 1, 1)])
                    scalars(NCH - 1)
                    outputs(NCH - 1)

        lay2 = ExitStack()
        R3 = sb(lay2, "R3b", [P, (J + 1) * D])
        with ExitStack() as ctx:
            pst, psb = ps(ctx, "pst14", [P, P]), ps(ctx, "psb14", [P, D])
            cs = chain_sems(ctx, "14")
            step14 = sem(ctx, "dve_14")
            with nc.Block() as block:
                @block.tensor
                def _(pe):
                    carries_pe(pe, cs, 0, D, R3[:, J * D:(J + 1) * D], pst, psb)

                @block.vector
                def _(dve):
                    ch = Chain(dve, step14)
                    feature_scan(ch, contD, R1, R3)
                    dve.sem_inc(cs[0], 1)
                    carries_dve(ch, cs, 0, D, ATD, pst, psb, carry[:, :], ALU.mult, ALU.add, 0.0)

        finish("l3", R2, R3, FD, sidxD, out)
        lay2.close()


def kernel(x, src, dst, edge_attr_10, edge_attr_3, edge_weight, L0_gnn_beta, L1_gnn_W1, L1_gnn_b1,
           L1_gnn_gamma1, L1_gnn_beta1, L1_gnn_W2, L1_gnn_b2, L1_gnn_gamma2, L1_gnn_beta2,
           L3_gnn_fc1_w1, L3_gnn_fc1_w2, L3_gnn_fc2_w1, L3_gnn_fc2_w2):
    import concourse.bacc as bacc
    from concourse.bass_utils import run_bass_kernel_spmd

    def edges(a, fill, shift=0):
        a = np.asarray(a)
        out = np.full((EP + 2,) + a.shape[1:], fill, a.dtype)
        out[0] = out[EP + 1] = -1 if shift else fill
        out[1:E + 1] = a
        return np.ascontiguousarray(out[1 + shift:1 + shift + EP].reshape((P, J) + a.shape[1:]))

    def row(a, n):
        return np.broadcast_to(np.resize(np.asarray(a), (1, n)), (P, n))

    arrays = {
        "x": np.asarray(x),
        "src": edges(src, N), "dst": edges(dst, N), "dst_prev": edges(dst, N, -1), "dst_next": edges(dst, N, 1),
        "attr3": edges(edge_attr_3, 1).reshape(P, J * 3),
        "attr10t": np.ascontiguousarray(edges(edge_attr_10, 0).transpose(2, 1, 0).reshape(10, J * P)),
        "weight": edges(edge_weight, 0),
        "W1": np.asarray(L1_gnn_W1), "W2": np.asarray(L1_gnn_W2),
        "vecs": np.ascontiguousarray(np.concatenate(
            [row(a, D) for a in (L1_gnn_b1, L1_gnn_gamma1, L1_gnn_beta1, L1_gnn_b2, L1_gnn_gamma2, L1_gnn_beta2,
                                 L0_gnn_beta)], axis=1)),
        "fc1_w1": np.asarray(L3_gnn_fc1_w1), "fc1_w2": np.asarray(L3_gnn_fc1_w2),
        "fc2_w1": np.asarray(L3_gnn_fc2_w1), "fc2_w2": np.asarray(L3_gnn_fc2_w2),
    }
    nc = bacc.Bacc("TRN2", target_bir_lowering=False, num_devices=1)
    t = {k: nc.dram_tensor("in_" + k, a.shape, mybir.dt.from_np(a.dtype), kind="ExternalInput").ap()
         for k, a in arrays.items()}
    out = nc.dram_tensor("out_rows", (N, D), F32, kind="ExternalOutput").ap()
    build(nc, t["x"], t["src"], t["dst"], t["dst_prev"], t["dst_next"], t["attr3"], t["attr10t"], t["weight"],
          None, t["W1"], t["W2"], t["vecs"], t["fc1_w1"], t["fc1_w2"], t["fc2_w1"], t["fc2_w2"], out)
    r = run_bass_kernel_spmd(nc, [{"in_" + k: a for k, a in arrays.items()}], core_ids=[0])
    return r.results[0]["out_rows"]
```
